# Optimizing a Trainium2 kernel written in Bass

```python
import numpy as np
import jax
import jax.numpy as jnp

def _softmax(x, axis=-1):
    return jax.nn.softmax(x, axis=axis)

def _gelu(x):
    return jax.nn.gelu(x, approximate=True)

def _silu(x):
    return jax.nn.silu(x)

def _sigmoid(x):
    return jax.nn.sigmoid(x)

def _layernorm(x, axis=-1, eps=1e-05):
    m = jnp.mean(x, axis=axis, keepdims=True)
    v = jnp.var(x, axis=axis, keepdims=True)
    return (x - m) / jnp.sqrt(v + eps)

def _scatter_add(tgt, idx, src, axis=0):
    return tgt.at[idx].add(src)

def _segment_sum(src, seg, n):
    return jax.ops.segment_sum(src, seg, n)
kernel_name = 'mk_flamingo_gated_d1_seqx_r2_dbfd85'

def setup_inputs(seed: int=0):
    np.random.seed(seed)
    _w = jnp.asarray

    def _rec_inputs():
        import jax
        import jax.numpy as jnp
        _rk = jax.random.key(seed)
        x = 7.22e-05 + 1 * jax.random.normal(jax.random.fold_in(_rk, 1), (1, 4096, 512), jnp.float32)
        _lenS = 4096 - jax.random.randint(jax.random.fold_in(_rk, 7), (1,), 0, max(1, 4096 // 4) + 1, jnp.int32)
        _lenS2 = 3202 - jax.random.randint(jax.random.fold_in(_rk, 8), (1,), 0, max(1, 3202 // 4) + 1, jnp.int32)
        _ctx_1024P = jax.random.normal(jax.random.fold_in(_rk, 11), (1, 16, 512), jnp.float32)
        _ctx_1024c = jax.random.dirichlet(jax.random.fold_in(_rk, 511), 0.3 * jnp.ones((16,), jnp.float32), (1, 3202))
        _ctx_1024t = jnp.einsum('bsk,bkd->bsd', _ctx_1024c, _ctx_1024P)
        _ctx_1024t = _ctx_1024t * jax.lax.rsqrt(jnp.mean(jnp.square(_ctx_1024t)) + 1e-12) * 0.953939
        ctx_1024 = -0.000514642 + 1.00011 * (_ctx_1024t + 0.3 * jax.random.normal(jax.random.fold_in(_rk, 611), (1, 3202, 512), jnp.float32))
        _g = jax.random.normal(jax.random.fold_in(_rk, 9001), (2, 1), jnp.float32)
        _g = jnp.sign(_g) * jnp.maximum(jnp.abs(_g), 1.0) + (_g == 0) * 1.0
        g_xattn = _g[0]
        g_ffn = _g[1]
        return (x, ctx_1024, g_xattn, g_ffn)
    x, ctx_1024, g_xattn, g_ffn = _rec_inputs()

    def _L0_xattn_setup():
        import jax, jax.numpy as jnp
        import numpy as np
        B, L_ENC, L_DEC, D = (16, 256, 128, 512)
        key = jax.random.key(seed)
        k1, k2, k3, k4, k5, k6 = jax.random.split(key, 6)
        encoder_hc = jax.random.normal(k1, (B, L_ENC, D), dtype=jnp.float32)
        decoder_hq = jax.random.normal(k2, (B, L_DEC, D), dtype=jnp.float32)
        w_sim = jax.random.normal(k3, (3 * D,), dtype=jnp.float32) * 0.02
        b_sim = jax.random.normal(k4, (1,), dtype=jnp.float32) * 0.02
        W_qv = jax.random.normal(k5, (4 * D, D), dtype=jnp.float32) * 0.02
        b_qv = jax.random.normal(k6, (D,), dtype=jnp.float32) * 0.02
        return {'encoder_hc': encoder_hc, 'decoder_hq': decoder_hq, 'w_sim': w_sim, 'b_sim': b_sim, 'W_qv': W_qv, 'b_qv': b_qv}
    _L0_xattn_all = _L0_xattn_setup()
    _L0_xattn_in = {k: v for k, v in _L0_xattn_all.items() if k in ('w_sim', 'b_sim', 'W_qv', 'b_qv')}
    del _L0_xattn_all

    def _L0_ffn_setup():
        import jax, jax.numpy as jnp
        import numpy as np
        B, T, D, F_FF, E, TOP_K = (8, 1024, 512, 2048, 8, 2)
        CAP_FACTOR = 1.25
        key = jax.random.key(seed)
        ks = jax.random.split(key, 7)
        s = 0.02
        return {'x': jax.random.normal(ks[0], (B, T, D), dtype=jnp.float32), 'w_router': jax.random.normal(ks[1], (D, E), dtype=jnp.float32) * s, 'b_router': jnp.zeros((E,), dtype=jnp.float32), 'w1': jax.random.normal(ks[2], (E, D, F_FF), dtype=jnp.float32) * s, 'b1': jnp.zeros((E, F_FF), dtype=jnp.float32), 'w2': jax.random.normal(ks[3], (E, F_FF, D), dtype=jnp.float32) * s, 'b2': jnp.zeros((E, D), dtype=jnp.float32)}
    _L0_ffn_all = _L0_ffn_setup()
    _L0_ffn_in = {k: v for k, v in _L0_ffn_all.items() if k in ('w_router', 'b_router', 'w1', 'b1', 'w2', 'b2')}
    del _L0_ffn_all
    return {'x': x, 'ctx_1024': ctx_1024, 'g_xattn': g_xattn, 'g_ffn': g_ffn, 'L0_xattn_w_sim': _L0_xattn_in['w_sim'], 'L0_xattn_b_sim': _L0_xattn_in['b_sim'], 'L0_xattn_W_qv': _L0_xattn_in['W_qv'], 'L0_xattn_b_qv': _L0_xattn_in['b_qv'], 'L0_ffn_w_router': _L0_ffn_in['w_router'], 'L0_ffn_b_router': _L0_ffn_in['b_router'], 'L0_ffn_w1': _L0_ffn_in['w1'], 'L0_ffn_b1': _L0_ffn_in['b1'], 'L0_ffn_w2': _L0_ffn_in['w2'], 'L0_ffn_b2': _L0_ffn_in['b2']}

def reference(x, ctx_1024, g_xattn, g_ffn, L0_xattn_w_sim, L0_xattn_b_sim, L0_xattn_W_qv, L0_xattn_b_qv, L0_ffn_w_router, L0_ffn_b_router, L0_ffn_w1, L0_ffn_b1, L0_ffn_w2, L0_ffn_b2):
    import jax
    import jax.numpy as jnp

    def _L0_xattn_ref(encoder_hc, decoder_hq, w_sim, b_sim, W_qv, b_qv):
        import jax, jax.numpy as jnp
        import numpy as np
        B, L_ENC, L_DEC, D = (16, 256, 128, 512)
        d = encoder_hc.shape[-1]
        w1, w2, w3 = (w_sim[:d], w_sim[d:2 * d], w_sim[2 * d:])
        Sim = (encoder_hc @ w1)[:, :, None] + (decoder_hq @ w2)[:, None, :] + jnp.einsum('bid,bjd->bij', encoder_hc * w3, decoder_hq) + b_sim[0]
        A = jax.nn.softmax(Sim, axis=2)
        hq_hat = jnp.einsum('bij,bjd->bid', A, decoder_hq)
        Batt = jax.nn.softmax(jnp.max(Sim, axis=2), axis=1)
        hc_bar = jnp.einsum('bi,bid->bd', Batt, encoder_hc)[:, None, :]
        hc_hat = jnp.broadcast_to(hc_bar, encoder_hc.shape)
        feats = jnp.concatenate([encoder_hc, hq_hat, encoder_hc * hq_hat, encoder_hc * hc_hat], axis=-1)
        hcq = feats @ W_qv + b_qv
        return hcq

    def _L0_ffn_ref(x, w_router, b_router, w1, b1, w2, b2):
        import jax, jax.numpy as jnp
        import numpy as np
        B, T, D, F_FF, E, TOP_K = (8, 1024, 512, 2048, 8, 2)
        CAP_FACTOR = 1.25
        b, t, d = x.shape
        n = b * t
        e = w_router.shape[1]
        xf = x.reshape(n, d)
        logits = xf.astype(jnp.float32) @ w_router + b_router
        gates = jax.nn.softmax(logits, axis=-1)
        topv, topi = jax.lax.top_k(gates, TOP_K)
        cap = max(1, int(CAP_FACTOR * n / e))
        e_flat = topi.reshape(-1)
        g_flat = topv.reshape(-1)
        tok = jnp.repeat(jnp.arange(n), TOP_K)
        onehot = jax.nn.one_hot(e_flat, e, dtype=jnp.int32)
        pos = jnp.cumsum(onehot, axis=0)[jnp.arange(n * TOP_K), e_flat] - 1
        keep = pos < cap
        posc = jnp.minimum(pos, cap - 1)
        buf = jnp.zeros((e, cap, d), x.dtype).at[e_flat, posc].add(jnp.where(keep[:, None], xf[tok], 0.0))
        h = jax.nn.gelu(jnp.einsum('ecd,edf->ecf', buf, w1) + b1[:, None, :], approximate=False)
        out = jnp.einsum('ecf,efd->ecd', h, w2) + b2[:, None, :]
        og = out[e_flat, posc]
        w = jnp.where(keep, g_flat, 0.0).astype(x.dtype)
        y = jnp.zeros((n, d), x.dtype).at[tok].add(w[:, None] * og)
        ws = jnp.zeros((n,), x.dtype).at[tok].add(w)
        y = jnp.where((ws > 0.0)[:, None], y / jnp.maximum(ws, 1e-06)[:, None], y)
        return y.reshape(b, t, d)
    x = x + jnp.tanh(g_xattn[0]) * _L0_xattn_ref(_layernorm(x, axis=-1), ctx_1024, L0_xattn_w_sim, L0_xattn_b_sim, L0_xattn_W_qv, L0_xattn_b_qv)
    x = x + jnp.tanh(g_ffn[0]) * _L0_ffn_ref(_layernorm(x, axis=-1), L0_ffn_w_router, L0_ffn_b_router, L0_ffn_w1, L0_ffn_b1, L0_ffn_w2, L0_ffn_b2)
    return x

_drawn_inputs = setup_inputs


def setup_inputs(seed=0):
    import zlib

    import numpy as np

    out = dict(_drawn_inputs(seed))
    spreads = {'L0_ffn_b_router': (0.0, 0.1), 'L0_ffn_b1': (0.0, 0.1), 'L0_ffn_b2': (0.0, 0.1)}
    factors = {}
    for name, (base, spread) in spreads.items():
        noise = np.random.default_rng([zlib.crc32(name.encode()), seed]).standard_normal(out[name].shape)
        drawn = base * np.exp(spread * noise) if base else spread * noise
        out[name] = jnp.asarray(drawn.astype(out[name].dtype))
    for name, factor in factors.items():
        out[name] = (out[name] * factor).astype(out[name].dtype)
    return out
```

```python
from contextlib import ExitStack

import concourse.bass as bass
from concourse import mybir

ALU = mybir.AluOpType
ACT = mybir.ActivationFunctionType
F32 = mybir.dt.float32
F16 = mybir.dt.float16
I32 = mybir.dt.int32
U32 = mybir.dt.uint32
AX = mybir.AxisListType
RMAX = bass.bass_isa.ReduceOp.max

P = 128
TOP = 14
EXPONENT = 0x7F800000
TINY = 2.0 ** -100
LN_SCALE = 2.0 ** 10
P_SCALE = 2.0 ** 15
LN_EPS = 1e-5
NEVER = -1e30


class Steps:

    def __init__(self, eng, sem, call, per, start=0):
        self.eng, self.sem, self.per, self.n = eng, sem, per, 0
        self.base = call * per + start

    def step(self, instruction):
        instruction.then_inc(self.sem, 1)
        self.n += 1
        assert self.n <= self.per

    def wait(self):
        self.eng.wait_ge(self.sem, self.base + self.n)

    def link(self, instruction):
        self.step(instruction)
        self.wait()


def apart(eng, passed):
    eng.sem_inc(passed, 1)


def bcast(ap, n):
    return ap[:, None, :].broadcast_to([ap.shape[0], n, ap.shape[1]])


def spread(ap, n):
    return ap[:, :, None].broadcast_to([ap.shape[0], ap.shape[1], n])


def cutter(arena):
    off = [0]

    def take(shape, dtype, at=None):
        n = 1
        for s in shape:
            n *= s
        words = n * (2 if dtype == F16 else 4) // 4
        a = off[0] if at is None else at
        if at is None:
            off[0] += words
        assert a + words <= arena.shape[1], (a + words, arena.shape)
        v = arena[:, a:a + words]
        if dtype != F32:
            v = v.bitcast(dtype)
        names = "abcdef"[:len(shape)]
        if len(shape) > 1:
            v = v.rearrange(f"p ({' '.join(names)}) -> p {' '.join(names)}",
                            **{names[i]: shape[i] for i in range(1, len(shape))})
        return v

    return take, off


def attention(nc, ps, arena, cst, x, ctx, w_sim, b_sim, feats, rows, hc_out):
    D = x.shape[1]
    KD = D // P
    NI, J = x.shape[0], ctx.shape[0]
    IB = 256
    NB = NI // IB
    QT = IB // P
    JT = -(-J // P)
    NP = JT // 2
    JR = J - (JT - 1) * P
    AHEAD = 5
    SLOTS = NP + AHEAD
    assert JT == 2 * NP

    take, off = cutter(arena)

    ctxT = take([2, KD, JT * P], F16)
    S = take([SLOTS, 2, IB], F32)
    at = off[0]
    ctxN = take([JT, 2, D], F16)
    raw = take([JT, D], F32, at)
    eT = take([2, 2, KD, IB], F16)
    qT = take([2, KD, IB], F16)
    prob = take([3, 2, 2, IB], F16)
    M = take([2, IB], F32)
    Mc = take([IB], F32)
    Mb = take([2, IB], F32)
    L = take([2, IB], F32)
    R = take([IB], F32)
    wrow = take([IB], F32)
    dg = take([2, QT, P], F32)
    xs = take([QT, D], F32)
    eh = take([QT, 2, D], F16)
    es = take([KD, P], F32)
    ehs = take([2, IB], F32)
    at = off[0]
    hq = take([KD, IB], F32)
    ch = take([2, 2, D], F16, at)
    feat = take([2, 2, KD, IB], F16)
    e32 = take([KD, IB], F32)
    w1b = take([D], F32)
    wcol = take([2, KD], F32)
    wq = take([2, KD], F32)
    wmx = take([2], F32)
    bound, qp2, qscale = take([1], F32), take([1], F32), take([1], F32)
    ew, ewt = take([NI // P], F32), take([QT], F32)
    cmax = take([JT], F32)
    gmax, gp2, gscale, sinv = (take([1], F32) for _ in range(4))
    pad, zero = take([1], F32), take([1], F32)
    bs = take([1], F32)
    stats, mv, sd, rs = take([QT, 6], F32), take([QT, 2], F32), take([QT], F32), take([QT], F32)
    m2 = take([2, QT], F32)
    top, new, neg, rr, ws = (take([1], F32) for _ in range(5))
    hcp = take([KD], F32)
    lneps = take([1], F32)
    blank = take([rows.shape[1]], F32)
    ident, identf, onesf = cst["ident"], cst["identf"], cst["onesf"]
    hc, wtot, cinv_g, cscale_g = hc_out["hc"], hc_out["wtot"], hc_out["ctx_inv"], hc_out["ctx_scale"]

    psS = ps[:, 0:2, :].rearrange("p s (h i) -> p s h i", h=2)
    psA = ps[:, 2:6, 0:IB]
    psT = [ps[:, 2 + h, :].bitcast(F16).rearrange("p (c i) -> p c i", i=P) for h in range(2)]
    psE = ps[:, 6, :].bitcast(F16).rearrange("p (c i) -> p c i", i=P)
    psL = ps[:, 6, 0:IB]
    psC = ps[:, 7, :]

    with ExitStack() as st:
        def sem(name):
            return st.enter_context(nc.semaphore(name))

        const_loaded, made, tail_zero, tail_loaded, setup = (sem(s) for s in (
            "const_loaded", "made", "tail_zero", "tail_loaded", "setup"))
        GROUPS = 5
        GT = (JT - 1) // GROUPS
        assert GT * GROUPS == JT - 1
        ctx_loaded = [sem(f"ctx_loaded_{g}") for g in range(GROUPS)]
        g_step, g_all, q_all = (sem(s) for s in ("g_step", "g_all", "q_all"))
        c_hi, c_lo, c_kept, ct_done, ct_act, ct_dve = (sem(s) for s in (
            "c_hi", "c_lo", "c_kept", "ct_done", "ct_act", "ct_dve"))
        x_loaded, ln_step, ln_sd, ln_hi, ln_t, et_ready, et_out, q_step, q_hi = (sem(s) for s in (
            "x_loaded", "ln_step", "ln_sd", "ln_hi", "ln_t", "et_ready", "et_out", "q_step", "q_hi"))
        qk_done, scores_ready, max_done, sub_done, exp_done, hi_done, p_ready, slot_free, av_done = (
            sem(s) for s in ("qk_done", "scores_ready", "max_done", "sub_done", "exp_done",
                             "hi_done", "p_ready", "slot_free", "av_done"))
        merge_done, mT_done, dg_step, mb_done, mb_ready, lsum_done, acc_step = (sem(s) for s in (
            "merge_done", "mT_done", "dg_step", "mb_done", "mb_ready", "lsum_done", "acc_step"))
        rows_blank = sem("rows_blank")
        f_hi, f_eh, f_lo, f_out = (sem(s) for s in ("f_hi", "f_eh", "f_lo", "f_out"))
        hc_step, hc_w, e_step = (sem(s) for s in ("hc_step", "hc_w", "e_step"))
        sp_passed, dve_passed = sem("sp_passed"), sem("dve_passed")
        block = st.enter_context(nc.Block())
        LK = 5 * QT + 2
        QK = QT * (KD + 2)
        ACK, HK, EK, DK = KD + 1, 5, 2 * KD, 2 * QT + 2

        @block.sync
        def _(sp):
            def load_x(b):
                sp.dma_start(xs, x[bass.ds(b * IB, IB), :].rearrange("(q p) d -> p q d", p=P))\
                    .then_inc(x_loaded, 16)

            def store_e(b):
                sp.wait_ge(et_ready, QT * b + QT)
                sp.dma_start(feats[bass.ds(b, 1), :, 0, :].rearrange("o p c -> (o p) c"),
                             eT[:, bass.ds(b % 2, 1)].rearrange("p o s k i -> p (o s k i)"))\
                    .then_inc(et_out, 16)
                sp.wait_ge(et_out, 16 * b + 16)

            def store_f(c):
                sp.wait_ge(f_lo, KD * c + KD)
                sp.dma_start(feats[bass.ds(c, 1), :, 1:3, :].rearrange("o p f c -> (o p) (f c)"),
                             feat.rearrange("p f s k i -> p (f s k i)")).then_inc(f_out, 16)
                sp.wait_ge(f_out, 16 * c + 32)
                apart(sp, sp_passed)

            sp.sem_inc(f_out, 16)
            for g in range(GROUPS):
                sp.dma_start(raw[:, g * GT:(g + 1) * GT, :],
                             ctx[g * GT * P:(g + 1) * GT * P, :].rearrange("(j p) d -> p j d", p=P))\
                    .then_inc(ctx_loaded[g], 16)
                if g == 0:
                    load_x(0)
                    with nc.allow_non_contiguous_dma("two columns of w_sim, once"):
                        for n in (1, 2):
                            sp.dma_start(wcol[:, n - 1, :], w_sim[n * D:(n + 1) * D].rearrange("(k p) -> p k", p=P))\
                                .then_inc(const_loaded, 16)
                    sp.dma_start(w1b, w_sim[0:D].partition_broadcast(P)).then_inc(const_loaded, 16)
                    sp.dma_start(bs, b_sim.partition_broadcast(P)).then_inc(const_loaded, 16)
            sp.wait_ge(tail_zero, 1)
            sp.dma_start(raw[0:JR, JT - 1, :], ctx[(JT - 1) * P:J, :]).then_inc(tail_loaded, 16)
            sp.wait_ge(made, 9)
            sp.dma_start(rows.rearrange("(t p) c -> p t c", p=P), bcast(blank, rows.shape[0] // P))\
                .then_inc(rows_blank, 16)
            for b in range(2):
                sp.wait_ge(ln_step, LK * (b + 1))
                load_x(b + 1)
                store_e(b)
            with sp.Fori(2, NB - 1) as b:
                sp.wait_ge(ln_step, LK * (b + 1))
                load_x(b + 1)
                store_e(b)
                store_f(b - 2)
            store_f(NB - 3)
            store_e(NB - 1)
            store_f(NB - 2)
            store_f(NB - 1)
            sp.wait_ge(rows_blank, 16)

        @block.gpsimd
        def _(pool):
            pool.memset(raw[:, JT - 1, :], 0.0).then_inc(tail_zero, 1)
            pool.memset(onesf, 1.0).then_inc(made, 1)
            pool.memset(identf, 0.0).then_inc(made, 1)
            pool.memset(pad, NEVER).then_inc(made, 1)
            pool.memset(zero, 0.0).then_inc(made, 1)
            pool.memset(lneps, LN_EPS / LN_SCALE ** 2).then_inc(made, 1)
            pool.memset(blank, 0.0).then_inc(made, 1)
            pool.wait_ge(made, 6)
            pool.iota(blank[:, D:D + 1].bitcast(U32), pattern=[[0, 1]], base=NI, channel_multiplier=0)\
                .then_inc(made, 1)
            pool.memset(pad[0:JR, :], 0.0).then_inc(made, 1)
            pool.affine_select(out=identf, in_=identf, compare_op=ALU.not_equal, fill=1.0, base=0,
                               pattern=[[-1, P]], channel_multiplier=1).then_inc(made, 1)
            pool.wait_ge(setup, 5)
            pool.partition_all_reduce(wmx, wmx, P, RMAX).then_inc(q_all, 1)
            pool.wait_ge(g_step, 1)
            pool.partition_all_reduce(gmax, gmax, P, RMAX).then_inc(g_all, 1)

        @block.vector
        def _(dve):
            def norm_stats(b):
                s = Steps(dve, ln_step, b, LK)
                dve.wait_ge(x_loaded, 16 * b + 16)
                for q in range(QT):
                    s.step(dve.bn_stats(stats[:, q, :], xs[:, q, :]))
                s.wait()
                apart(dve, dve_passed)
                for q in range(QT):
                    s.step(dve.bn_aggr(mv[:, q, :], stats[:, q, :]))

            def norm(b):
                s = Steps(dve, ln_step, b, LK)
                s.n = 2 * QT
                dve.wait_ge(ln_sd, b + 1)
                s.link(dve.reciprocal(rs, sd))
                for q in range(QT):
                    s.step(dve.tensor_scalar(xs[:, q, :], xs[:, q, :], mv[:, q, 0:1], rs[:, q:q + 1],
                                             ALU.subtract, ALU.mult))

            def norm_lo(b):
                s = Steps(dve, ln_step, b, LK)
                s.n = 3 * QT + 1
                for q in range(QT):
                    dve.wait_ge(ln_hi, QT * b + q + 1)
                    s.step(dve.tensor_tensor(eh[:, q, 1, :], xs[:, q, :], eh[:, q, 0, :], ALU.subtract))
                for q in range(QT):
                    s.step(dve.tensor_tensor_reduce(out=xs[:, q, :], in0=xs[:, q, :], in1=w1b,
                                                    scale=1 / LN_SCALE, scalar=bs[:, 0:1], op0=ALU.mult,
                                                    op1=ALU.add, accum_out=ewt[:, q:q + 1]))
                s.wait()
                s.step(dve.tensor_copy(ew[:, bass.ds(b * QT, QT)], ewt))

            def query(b, q):
                s = Steps(dve, q_step, b, QK)
                s.n = q * (KD + 2)
                et = eT[:, bass.ds(b % 2, 1)].rearrange("p o s k i -> p (o s) k i")[:, :, :, q * P:(q + 1) * P]
                dve.wait_ge(et_ready, QT * b + q + 1)
                if q:
                    s.wait()
                s.link(dve.tensor_tensor(es, et[:, 0], et[:, 1], ALU.add))
                for k in range(KD):
                    s.step(dve.tensor_scalar(es[:, k, :], es[:, k, :], wq[:, 1, k:k + 1], wq[:, 0, k:k + 1],
                                             ALU.mult, ALU.add))
                dve.wait_ge(q_hi, QT * b + q + 1)
                s.step(dve.tensor_tensor(qT[:, 1, :, q * P:(q + 1) * P], es, qT[:, 0, :, q * P:(q + 1) * P],
                                         ALU.subtract))

            def scale_of(s, sc, p2, m):
                s.link(dve.tensor_scalar(p2.bitcast(I32), m.bitcast(I32), EXPONENT, None, ALU.bitwise_and))
                s.link(dve.tensor_scalar(sc.bitcast(I32), p2.bitcast(I32), -1, float((254 + TOP) << 23),
                                         ALU.mult, ALU.add))

            def running_max(b, t):
                n = b * NP + t
                dve.wait_ge(scores_ready, n + 3)
                if t == 0:
                    dve.tensor_copy(M, slot_of(n)).then_inc(max_done, 1)
                else:
                    dve.wait_ge(max_done, n)
                    dve.tensor_tensor(M, M, slot_of(n), ALU.max).then_inc(max_done, 1)

            def slot_of(a):
                return S[:, bass.ds(a % SLOTS, 1)].rearrange("p o h i -> p (o h) i")

            def split_pair(t):
                for h in range(2):
                    j = 2 * t + h
                    dve.wait_ge(c_hi, j + 1)
                    dve.scalar_tensor_tensor(out=ch[:, h, 1, :], in0=raw[:, j, :], scalar=gscale[:, 0:1],
                                             in1=ch[:, h, 0, :], op0=ALU.mult, op1=ALU.subtract)\
                       .then_inc(c_lo, 1)
                for h in range(2):
                    j = 2 * t + h
                    dve.wait_ge(c_lo, j + 1)
                    dve.tensor_copy(ctxN[:, j], ch[:, h]).then_inc(c_kept, 1)
                dve.wait_ge(ct_done, 2 * t + 4)
                dve.tensor_copy(ctxT[:, :, :, (2 * t + 1) * P:(2 * t + 2) * P],
                                psT[1].rearrange("p (s k) i -> p s k i", s=2)).then_inc(ct_dve, 1)

            def subtract(a):
                dve.tensor_tensor(slot_of(a), slot_of(a), bcast(Mb[:, 0, :], 2), ALU.subtract)\
                   .then_inc(sub_done, 1)

            def low_and_sum(a, first):
                dve.wait_ge(hi_done, a + 1)
                pr = prob[:, bass.ds(a % 3, 1)].rearrange("p o s h i -> p (o s) h i")
                dve.scalar_tensor_tensor(out=pr[:, 1], in0=slot_of(a), scalar=P_SCALE, in1=pr[:, 0],
                                         op0=ALU.mult, op1=ALU.subtract).then_inc(p_ready, 1)
                if first:
                    dve.tensor_copy(L, slot_of(a)).then_inc(slot_free, 1)
                else:
                    dve.wait_ge(slot_free, SLOTS + a)
                    dve.tensor_tensor(L, L, slot_of(a), ALU.add).then_inc(slot_free, 1)

            def maxima(c):
                dve.wait_ge(max_done, NP * (c + 1))
                dve.tensor_tensor(Mc, M[:, 0, :], M[:, 1, :], ALU.max).then_inc(merge_done, 1)
                dve.wait_ge(mT_done, c + 1)
                s = Steps(dve, dg_step, c, DK)
                s.link(dve.tensor_reduce(m2[:, 0, :], psC[:, 0:IB].rearrange("p (q i) -> p q i", q=QT),
                                         AX.X, ALU.max))
                s.link(dve.tensor_tensor(m2[:, 1, :], m2[:, 0, :], ew[:, bass.ds(c * QT, QT)], ALU.add))
                for n in range(2):
                    for q in range(QT):
                        s.step(dve.tensor_scalar(dg[:, n, q, :], identf, m2[:, n, q:q + 1], None, ALU.mult))

            def take_acc(c):
                s = Steps(dve, acc_step, c, ACK)
                dve.wait_ge(lsum_done, c + 1)
                s.link(dve.reciprocal(R, psL))
                dve.wait_ge(av_done, NP * (c + 1) + 3)
                for k in range(KD):
                    s.step(dve.scalar_tensor_tensor(out=hq[:, k, :], in0=psA[:, k, :], scalar=1 / P_SCALE,
                                                    in1=R, op0=ALU.mult, op1=ALU.mult))

            def products(c, k):
                dve.wait_ge(acc_step, ACK * (c + 1))
                dve.wait_ge(e_step, EK * (c + 1))
                if k >= 2:
                    dve.wait_ge(f_lo, KD * c + k - 1)
                dve.scalar_tensor_tensor(out=ehs[:, k % 2, :], in0=hq[:, k, :], scalar=1 / LN_SCALE / 32,
                                         in1=e32[:, k, :], op0=ALU.mult, op1=ALU.mult).then_inc(f_eh, 1)

            def lows(c, k):
                n = KD * c + k
                dve.wait_ge(f_hi, 2 * n + 1)
                dve.tensor_tensor(feat[:, 0, 1, k, :], hq[:, k, :], feat[:, 0, 0, k, :], ALU.subtract)
                dve.wait_ge(f_hi, 2 * n + 2)
                dve.tensor_tensor(feat[:, 1, 1, k, :], ehs[:, k % 2, :], feat[:, 1, 0, k, :], ALU.subtract)\
                   .then_inc(f_lo, 1)

            def pool_top(c):
                s = Steps(dve, hc_step, c, HK)
                s.link(dve.tensor_reduce(new, Mb[:, 1, :], AX.X, ALU.max))
                s.link(dve.tensor_tensor(new, new, top, ALU.max))
                s.step(dve.tensor_scalar(neg, new, -1.0, None, ALU.mult))

            def pool_part(c, k):
                s = Steps(dve, e_step, c, EK)
                s.n = 2 * k
                et = eT[:, bass.ds(c % 2, 1)].rearrange("p o s k i -> p (o s) k i")
                if k:
                    s.wait()
                s.link(dve.tensor_tensor(e32[:, k, :], et[:, 0, k, :], et[:, 1, k, :], ALU.add))
                if k == 0:
                    dve.wait_ge(hc_w, 2 * c + 2)
                s.step(dve.tensor_tensor_reduce(out=Mc, in0=e32[:, k, :], in1=wrow, scale=1.0, scalar=0.0,
                                                op0=ALU.mult, op1=ALU.add, accum_out=hcp[:, k:k + 1]))

            def pool_update(c):
                s = Steps(dve, hc_step, c, HK)
                s.n = 3
                dve.wait_ge(e_step, EK * (c + 1))
                dve.tensor_copy(top, new)
                s.step(dve.scalar_tensor_tensor(out=hc, in0=hc, scalar=rr[:, 0:1], in1=hcp,
                                                op0=ALU.mult, op1=ALU.add))
                s.link(dve.scalar_tensor_tensor(out=wtot, in0=wtot, scalar=rr[:, 0:1], in1=ws,
                                                op0=ALU.mult, op1=ALU.add))

            def iteration(b, first=False, last=False, norms=True):
                maxima(b - 1)
                if not first:
                    take_acc(b - 2)
                if not last:
                    running_max(b, 0)
                dve.wait_ge(mb_ready, b)
                a0 = NP * (b - 1)
                subtract(a0)
                subtract(a0 + 1)
                subtract(a0 + 2)
                if not last:
                    running_max(b, 1)
                low_and_sum(a0, True)
                pool_top(b - 1)
                if not last:
                    for t in range(2, AHEAD):
                        running_max(b, t)
                for t in range(NP):
                    if t + 1 < NP:
                        low_and_sum(a0 + t + 1, False)
                    if t + 3 < NP:
                        subtract(a0 + t + 3)
                    if not last and t + AHEAD < NP:
                        running_max(b, t + AHEAD)
                    if not first and t < KD:
                        products(b - 2, t)
                    if not first and 1 <= t <= KD:
                        lows(b - 2, t - 1)
                    if KD <= t < 2 * KD:
                        pool_part(b - 1, t - KD)
                    if t == 2 * KD:
                        pool_update(b - 1)
                    if norms:
                        if t == 1:
                            norm_stats(b + 1)
                        if t == 4:
                            norm(b + 1)
                        if t == 5:
                            norm_lo(b + 1)
                        if 11 <= t < 11 + QT:
                            query(b + 1, t - 11)

            dve.sem_inc(slot_free, SLOTS)
            dve.memset(top, NEVER).then_inc(setup, 1)
            dve.memset(hc, 0.0).then_inc(setup, 1)
            dve.memset(wtot, 0.0).then_inc(setup, 1)
            dve.wait_ge(made, 9)
            dve.tensor_copy(ident, identf).then_inc(setup, 1)
            dve.wait_ge(const_loaded, 64)
            dve.tensor_reduce(wmx, wcol, AX.X, ALU.max, apply_absolute_value=True).then_inc(setup, 1)
            norm_stats(0)
            s = Steps(dve, setup, 0, 11)
            s.n = 5
            dve.wait_ge(q_all, 1)
            s.link(dve.scalar_tensor_tensor(out=bound, in0=wmx[:, 1:2], scalar=32.0, in1=wmx[:, 0:1],
                                            op0=ALU.mult, op1=ALU.add))
            s.link(dve.tensor_scalar(bound, bound, TINY, None, ALU.max))
            scale_of(s, qscale, qp2, bound)
            s.step(dve.tensor_scalar(wq[:, 0, :], wcol[:, 0, :], qscale[:, 0:1], None, ALU.mult))
            s.link(dve.tensor_scalar(wq[:, 1, :], wcol[:, 1, :], qscale[:, 0:1], 1 / LN_SCALE, ALU.mult, ALU.mult))
            norm(0)
            norm_lo(0)
            for g in range(GROUPS):
                dve.wait_ge(ctx_loaded[g], 16)
                dve.tensor_reduce(cmax[:, g * GT:(g + 1) * GT], raw[:, g * GT:(g + 1) * GT, :], AX.X, ALU.max,
                                  apply_absolute_value=True)
                if g == 0:
                    for q in range(QT):
                        query(0, q)
            dve.wait_ge(tail_loaded, 16)
            dve.tensor_reduce(cmax[:, JT - 1:JT], raw[:, JT - 1, :], AX.X, ALU.max,
                              apply_absolute_value=True).then_inc(setup, 1)
            dve.wait_ge(setup, 12)
            s = Steps(dve, g_step, 0, 7)
            s.step(dve.tensor_reduce(gmax, cmax, AX.X, ALU.max))
            dve.wait_ge(g_all, 1)
            s.link(dve.tensor_scalar(gmax, gmax, TINY, None, ALU.max))
            scale_of(s, gscale, gp2, gmax)
            s.step(dve.tensor_copy(cscale_g, gscale))
            s.link(dve.tensor_scalar(cinv_g, gp2, 2.0 ** -TOP, None, ALU.mult))
            s.link(dve.tensor_scalar(sinv, qp2, cinv_g, 2.0 ** -TOP, ALU.mult, ALU.mult))
            split_pair(0)
            for t in range(NP):
                if t + 1 < NP:
                    split_pair(t + 1)
                if t >= 1:
                    running_max(0, t - 1)
                if t == 1:
                    norm_stats(1)
                if t == 3:
                    norm(1)
                if t == 4:
                    norm_lo(1)
            running_max(0, NP - 1)
            for q in range(QT):
                query(1, q)
            iteration(1, first=True)
            with dve.Fori(2, NB - 1) as b:
                iteration(b)
            iteration(NB - 1, norms=False)
            iteration(NB, last=True, norms=False)
            take_acc(NB - 1)
            for k in range(KD):
                products(NB - 1, k)
                lows(NB - 1, k)

        @block.scalar
        def _(act):
            def split_pair(t):
                for h in range(2):
                    j = 2 * t + h
                    if t:
                        act.wait_ge(ct_done, j + 1)
                        act.wait_ge(c_kept, j - 1)
                    act.activation(ch[:, h, 0, :], raw[:, j, :], ACT.Identity, bias=zero[:, 0:1],
                                   scale=gscale[:, 0:1]).then_inc(c_hi, 1)

            def turned(t):
                act.wait_ge(ct_done, 2 * t + 3)
                act.copy(ctxT[:, :, :, 2 * t * P:(2 * t + 1) * P],
                         psT[0].rearrange("p (s k) i -> p s k i", s=2)).then_inc(ct_act, 1)

            def norm_sd(b):
                act.wait_ge(ln_step, LK * b + 2 * QT)
                act.activation(sd, mv[:, :, 1], ACT.Sqrt, bias=lneps[:, 0:1], scale=1 / LN_SCALE ** 2)\
                   .then_inc(ln_sd, 1)

            def norm_hi(b):
                for q in range(QT):
                    act.wait_ge(ln_step, LK * b + 2 * QT + 2 + q)
                    act.copy(eh[:, q, 0, :], xs[:, q, :]).then_inc(ln_hi, 1)

            def norm_turned(b, old):
                if old:
                    act.wait_ge(et_out, 16 * (b - 1))
                    act.wait_ge(e_step, EK * (b - 1))
                et = eT[:, bass.ds(b % 2, 1)].rearrange("p o s k i -> p (o s k) i")
                for q in range(QT):
                    act.wait_ge(ln_t, QT * b + q + 1)
                    act.copy(et[:, :, q * P:(q + 1) * P], psE).then_inc(et_ready, 1)

            def query_hi(b, q, old):
                if old and q == 0:
                    act.wait_ge(qk_done, NP * b)
                act.wait_ge(q_step, QK * b + (KD + 2) * q + KD + 1)
                act.copy(qT[:, 0, :, q * P:(q + 1) * P], es).then_inc(q_hi, 1)

            def scores(b, t):
                n = b * NP + t
                act.wait_ge(qk_done, n + 1)
                act.wait_ge(slot_free, n + 1)
                slot = S[:, bass.ds(n % SLOTS, 1)].rearrange("p o h i -> p (o h) i")
                bank = psS[:, bass.ds(n % 2, 1)].rearrange("p o h i -> p (o h) i")
                if t < NP - 1:
                    act.activation(slot, bank, ACT.Identity, bias=zero[:, 0:1], scale=sinv[:, 0:1])\
                       .then_inc(scores_ready, 1)
                else:
                    act.activation(slot[:, 0, :], bank[:, 0, :], ACT.Identity, bias=zero[:, 0:1], scale=sinv[:, 0:1])
                    act.activation(slot[:, 1, :], bank[:, 1, :], ACT.Identity, bias=pad[:, 0:1], scale=sinv[:, 0:1])\
                       .then_inc(scores_ready, 1)

            def probabilities(a):
                slot = S[:, bass.ds(a % SLOTS, 1)].rearrange("p o h i -> p (o h) i")
                act.wait_ge(sub_done, a + 1)
                act.activation(slot, slot, ACT.Exp).then_inc(exp_done, 1)
                act.wait_ge(av_done, a + 1)
                act.wait_ge(exp_done, a + 1)
                act.activation(prob[:, bass.ds(a % 3, 1), 0].rearrange("p o h i -> p (o h) i"), slot,
                               ACT.Copy, scale=P_SCALE).then_inc(hi_done, 1)

            def high_hq(c, k):
                if k == 0:
                    act.wait_ge(acc_step, ACK * (c + 1))
                    act.wait_ge(f_out, 16 * (c + 1))
                act.copy(feat[:, 0, 0, k, :], hq[:, k, :]).then_inc(f_hi, 1)

            def high_eh(c, k):
                act.wait_ge(f_eh, KD * c + k + 1)
                act.copy(feat[:, 1, 0, k, :], ehs[:, k % 2, :]).then_inc(f_hi, 1)

            def iteration(b, first=False, last=False, norms=True):
                a0 = NP * (b - 1)
                if not last:
                    scores(b, 0)
                act.wait_ge(mb_done, b)
                act.copy(Mb, psC.rearrange("p (n i) -> p n i", n=2)).then_inc(mb_ready, 1)
                probabilities(a0)
                if not last:
                    scores(b, 1)
                probabilities(a0 + 1)
                if not last:
                    for t in range(2, AHEAD):
                        scores(b, t)
                act.wait_ge(hc_step, HK * (b - 1) + 3)
                act.activation(rr, top, ACT.Exp, bias=neg[:, 0:1]).then_inc(hc_w, 1)
                act.activation(wrow, Mb[:, 1, :], ACT.Exp, bias=neg[:, 0:1], accum_out=ws).then_inc(hc_w, 1)
                for t in range(NP):
                    if t + 2 < NP:
                        probabilities(a0 + t + 2)
                    if not last and t + AHEAD < NP:
                        scores(b, t + AHEAD)
                    if not first and t < KD:
                        high_hq(b - 2, t)
                        high_eh(b - 2, t)
                    if norms:
                        if t == 2:
                            norm_sd(b + 1)
                        if t == 4:
                            norm_hi(b + 1)
                        if t == 9:
                            norm_turned(b + 1, True)
                        if 11 <= t < 11 + QT:
                            query_hi(b + 1, t - 11, True)

            act.sem_inc(scores_ready, 2)
            act.wait_ge(made, 9)
            norm_sd(0)
            norm_hi(0)
            norm_turned(0, False)
            for q in range(QT):
                query_hi(0, q, False)
            act.wait_ge(g_step, 7)
            split_pair(0)
            for t in range(NP):
                if t + 1 < NP:
                    split_pair(t + 1)
                turned(t)
                if t >= 1:
                    scores(0, t - 1)
                if t == 2:
                    norm_sd(1)
                if t == 4:
                    norm_hi(1)
                if t == 6:
                    norm_turned(1, False)
            scores(0, NP - 1)
            for q in range(QT):
                query_hi(1, q, True)
            iteration(1, first=True)
            with act.Fori(2, NB - 1) as b:
                iteration(b)
            iteration(NB - 1, norms=False)
            iteration(NB, last=True, norms=False)
            for k in range(KD):
                high_hq(NB - 1, k)
                high_eh(NB - 1, k)

        @block.tensor
        def _(pe):
            def turn_e(b):
                for q in range(QT):
                    pe.wait_ge(ln_step, LK * b + 3 * QT + 2 + q)
                    if q:
                        pe.wait_ge(et_ready, QT * b + q)
                    for s in range(2):
                        for k in range(KD):
                            mm = pe.transpose(psE[:, s * KD + k, :], eh[:, q, s, k * P:(k + 1) * P], ident)
                    mm.then_inc(ln_t, 1)

            def turn_ctx(t):
                for h in range(2):
                    pe.wait_ge(c_lo, 2 * t + h + 1)
                    if t:
                        pe.wait_ge((ct_act, ct_dve)[h], t)
                    for s in range(2):
                        for k in range(KD):
                            mm = pe.transpose(psT[h][:, s * KD + k, :], ch[:, h, s, k * P:(k + 1) * P], ident)
                    mm.then_inc(ct_done, 1)

            def scores(b, t):
                n = b * NP + t
                pe.wait_ge(scores_ready, n + 1)
                for h in range(2):
                    out = psS[:, bass.ds(n % 2, 1), h, :].rearrange("p o i -> p (o i)")
                    for k in range(KD):
                        for s, r in ((0, 0), (0, 1), (1, 0)):
                            mm = pe.matmul(out, ctxT[:, s, k, (2 * t + h) * P:(2 * t + h + 1) * P], qT[:, r, k, :],
                                           start=(k == 0 and s + r == 0), stop=(k == KD - 1 and s == 1))
                mm.then_inc(qk_done, 1)

            def products(b, t):
                a = (b - 1) * NP + t
                pe.wait_ge(p_ready, a + 1)
                for h in range(2):
                    for k in range(KD):
                        for s, r in ((0, 0), (0, 1), (1, 0)):
                            mm = pe.matmul(
                                psA[:, k, :], ctxN[:, 2 * t + h, s, k * P:(k + 1) * P],
                                prob[:, bass.ds(a % 3, 1), r, h, :].rearrange("p o i -> p (o i)"),
                                start=(t + h + s + r == 0), stop=(t == NP - 1 and h == 1 and s == 1))
                mm.then_inc(av_done, 1)

            def sums(c):
                pe.wait_ge(slot_free, SLOTS + NP * (c + 1))
                for h in range(2):
                    mm = pe.matmul(psL, onesf, L[:, h, :], start=(h == 0), stop=(h == 1))
                mm.then_inc(lsum_done, 1)

            def iteration(b, first=False, last=False, norms=True):
                pe.wait_ge(merge_done, b)
                for q in range(QT):
                    mm = pe.transpose(psC[:, q * P:(q + 1) * P], Mc[:, q * P:(q + 1) * P], identf)
                mm.then_inc(mT_done, 1)
                if not last:
                    pe.wait_ge(q_step, QK * (b + 1))
                    scores(b, 0)
                pe.wait_ge(dg_step, DK * b)
                pe.matmul(psC, onesf, dg.rearrange("p n q i -> p (n q i)"), start=True, stop=True)\
                  .then_inc(mb_done, 1)
                if not first:
                    sums(b - 2)
                if not last:
                    for t in range(1, AHEAD):
                        scores(b, t)
                if not first:
                    pe.wait_ge(acc_step, ACK * (b - 1))
                if first:
                    pe.wait_ge(c_kept, JT)
                for t in range(NP):
                    products(b, t)
                    if not last and t + AHEAD < NP:
                        scores(b, t + AHEAD)
                    if norms and t == 8:
                        turn_e(b + 1)

            pe.sem_inc(av_done, 3)
            pe.sem_inc(ct_done, 2)
            pe.wait_ge(setup, 4)
            turn_e(0)
            turn_ctx(0)
            for t in range(NP):
                if t + 1 < NP:
                    turn_ctx(t + 1)
                pe.wait_ge(ct_act, t + 1)
                pe.wait_ge(ct_dve, t + 1)
                if t == 0:
                    pe.wait_ge(q_step, QK)
                scores(0, t)
                if t == 5:
                    turn_e(1)
            iteration(1, first=True)
            with pe.Fori(2, NB - 1) as b:
                iteration(b)
            iteration(NB - 1, norms=False)
            iteration(NB, last=True, norms=False)
            sums(NB - 1)


def merge_and_route(nc, ps, arena, cst, x, w_qv, b_qv, g_x, g_f, w_r, b_r, feats, rows, x1_out, hc_in):
    D = x.shape[1]
    KD = D // P
    NI = x.shape[0]
    IB = 256
    NB, QT = NI // IB, IB // P
    E = w_r.shape[1]
    CAP = rows.shape[0] // E
    NS = E * CAP
    FT = 3 * KD
    ROW = rows.shape[1]
    FAR = 8192.0
    take, _ = cutter(arena)

    Wt = take([FT, 2, D], F16)
    ft = [take([3, 2, KD, IB], F16) for _ in range(2)]
    W = take([4 * KD, D], F32)
    x2 = [take([QT, D], F32) for _ in range(2)]
    xn = take([QT, D], F32)
    row = [take([QT, ROW], F32) for _ in range(2)]
    halves = [r.bitcast(F16) for r in row]
    xT = take([QT, 2, KD, P], F16)
    bqb, brb = take([D], F32), take([E], F32)
    wr, wrs = take([KD, E], F32), take([KD, 2, E], F16)
    mx = take([5], F32)
    u, up2, sig, rp2, rsc = (take([1], F32) for _ in range(5))
    sc3 = take([3], F32)
    cY, cR, tx, tf, rw = (take([1], F32) for _ in range(5))
    gx, gf = take([1], F32), take([1], F32)
    hcn = take([KD], F32)
    t1 = take([2], F32)
    stats, mv, sd, rs = take([QT, 6], F32), take([QT, 2], F32), take([QT], F32), take([QT], F32)
    lneps = take([1], F32)
    iota8, tok = take([E], F32), take([NI // P], U32)
    lg, ex, gt = take([QT, E], F32), take([QT, E], F32), take([QT, E], F32)
    lm, lsum, lr = take([QT], F32), take([QT], F32), take([QT], F32)
    m8, ix = take([QT, 8], F32), take([QT, 8], U32)
    ixf = take([2, QT], F32)
    oh = take([2, QT, E], F32)
    mask = take([QT, E], F16)
    count = take([E], F32)
    base, pos, ohp = take([QT, E], F32), take([QT, E], F32), take([2, QT, E], F32)
    pk, kp, dst, away = (take([2, QT], F32) for _ in range(4))
    dsti = [take([2, QT], U32) for _ in range(2)]
    wk, wsum, wi = take([2, QT], F32), take([QT], F32), take([QT], F32)
    tri, ones = take([P], F16), take([P], F16)
    trif = take([P], F32)
    ident = cst["ident"]
    hc, wtot, cinv, cscale = hc_in["hc"], hc_in["wtot"], hc_in["ctx_inv"], hc_in["ctx_scale"]

    psY = ps[:, 0:2, :]
    psR = ps[:, 2, :].bitcast(F16).rearrange("p (c i) -> p c i", i=P)
    psG = ps[:, 3, 0:QT * E].rearrange("p (i e) -> p i e", e=E)
    psK = ps[:, 4, 0:2 * QT * E].rearrange("p (n e) -> p n e", e=E)

    with ExitStack() as st:
        def sem(name):
            return st.enter_context(nc.semaphore(name))

        w_loaded, p_loaded, made, mx_done, mx_all, prep, w_hi, w_lo, t_done = (sem(s) for s in (
            "w_loaded", "p_loaded", "made2", "mx_done", "mx_all", "prep", "w_hi", "w_lo", "t_done"))
        f_loaded = [sem("f_loaded_0"), sem("f_loaded_1")]
        x_loaded = [sem("x2_loaded_0"), sem("x2_loaded_1")]
        x_stored = [sem("x1_stored_0"), sem("x1_stored_1")]
        y_done, y_step, sd_done, hi_done, turned, xt_ready, logits, e_done, r_step, counted = (sem(s) for s in (
            "y_done", "y_step", "sd_done", "row_hi", "turned", "xt_ready", "logits", "e_done", "r_step",
            "counted"))
        sent, row_free = [[sem(f"{name}_{v}") for v in range(2)] for name in ("sent", "row_free")]
        sp_passed, dve_passed, pool_passed = (sem(f"{e}_passed_2") for e in ("sp", "dve", "pool"))
        block = st.enter_context(nc.Block())
        YK = 2 * QT + 2 * QT + 1 + 2 * QT
        R1 = 9 + 2 * QT
        RK = R1 + 17 + QT

        @block.sync
        def _(sp):
            sp.dma_start(W, w_qv.rearrange("(c p) d -> p c d", p=P)).then_inc(w_loaded, 16)
            sp.dma_start(bqb, b_qv.partition_broadcast(P)).then_inc(p_loaded, 16)
            sp.dma_start(brb, b_r.partition_broadcast(P)).then_inc(p_loaded, 16)
            sp.dma_start(gx, g_x.partition_broadcast(P)).then_inc(p_loaded, 16)
            sp.dma_start(gf, g_f.partition_broadcast(P)).then_inc(p_loaded, 16)
            sp.dma_start(wr, w_r.rearrange("(k p) e -> p k e", p=P)).then_inc(p_loaded, 16)

            def load(b, v):
                sp.dma_start(ft[v].rearrange("p f s k i -> p (f s k i)"),
                             feats[bass.ds(b, 1)].rearrange("o p f c -> (o p) (f c)")).then_inc(f_loaded[v], 16)
                sp.dma_start(x2[v], x[bass.ds(b * IB, IB), :].rearrange("(q p) d -> p q d", p=P))\
                    .then_inc(x_loaded[v], 16)

            def store(b, v, n):
                sp.wait_ge(y_step, YK * b + 2 * QT)
                apart(sp, sp_passed)
                sp.dma_start(x1_out[bass.ds(b * IB, IB), :].rearrange("(q p) d -> p q d", p=P), x2[v])\
                    .then_inc(x_stored[v], 16)
                sp.wait_ge(x_stored[v], 16 * (n + 1))
                apart(sp, sp_passed)

            load(0, 0)
            load(1, 1)
            with sp.Fori(0, NB // 2 - 1) as n:
                for v in range(2):
                    store(2 * n + v, v, n)
                    sp.wait_ge(y_step, YK * (2 * n + v + 1))
                    apart(sp, sp_passed)
                    sp.wait_ge(y_done, QT * (2 * n + v + 1))
                    load(2 * n + v + 2, v)
            for v in range(2):
                store(NB - 2 + v, v, NB // 2 - 1)

        @block.gpsimd
        def _(pool):
            pool.memset(lneps, LN_EPS / LN_SCALE ** 2).then_inc(made, 1)
            pool.memset(trif, 1.0).then_inc(made, 1)
            pool.iota(tok, pattern=[[P, NI // P]], base=0, channel_multiplier=1).then_inc(made, 1)
            pool.iota(iota8, pattern=[[1, E]], base=0, channel_multiplier=0,
                      allow_small_or_imprecise_dtypes=True).then_inc(made, 1)
            pool.wait_ge(made, 4)
            pool.affine_select(out=trif, in_=trif, compare_op=ALU.is_gt, fill=0.0, base=0,
                               pattern=[[1, P]], channel_multiplier=-1).then_inc(made, 1)
            pool.sem_inc(row_free[0], 1)
            pool.sem_inc(row_free[1], 1)
            pool.wait_ge(mx_done, 5)
            pool.partition_all_reduce(mx, mx, P, RMAX).then_inc(mx_all, 1)
            with pool.Fori(0, NB // 2) as n:
                for v in range(2):
                    pool.wait_ge(r_step, RK * (2 * n + v + 1))
                    apart(pool, pool_passed)
                    for q in range(QT):
                        for k in range(2):
                            pool.indirect_dma_start(
                                out=rows, out_offset=bass.IndirectOffsetOnAxis(ap=dsti[v][:, k, q:q + 1], axis=0),
                                in_=row[v][:, q, :], in_offset=None, bounds_check=NS - 1, oob_is_err=False)\
                                .then_inc(sent[v], 16)
                    pool.wait_ge(sent[v], 32 * QT * (n + 1))
                    pool.sem_inc(row_free[v], 1)

        @block.vector
        def _(dve):
            def y_part(b, v, q):
                s = Steps(dve, y_step, b, YK)
                s.n = 2 * q
                dve.wait_ge(y_done, QT * b + q + 1)
                s.link(dve.tensor_tensor(x2[v][:, q, :], x2[v][:, q, :], bqb, ALU.add))
                s.step(dve.scalar_tensor_tensor(out=x2[v][:, q, :], in0=psY[:, q, :], scalar=cY[:, 0:1],
                                                in1=x2[v][:, q, :], op0=ALU.mult, op1=ALU.add))

            def norm_part(b, v, n):
                s = Steps(dve, y_step, b, YK)
                s.n = 2 * QT
                s.wait()
                for q in range(QT):
                    s.step(dve.bn_stats(stats[:, q, :], x2[v][:, q, :]))
                s.wait()
                apart(dve, dve_passed)
                for q in range(QT):
                    s.step(dve.bn_aggr(mv[:, q, :], stats[:, q, :]))
                dve.wait_ge(sd_done, b + 1)
                s.link(dve.reciprocal(rs, sd))
                for q in range(QT):
                    s.step(dve.tensor_scalar(xn[:, q, :], x2[v][:, q, :], mv[:, q, 0:1], rs[:, q:q + 1],
                                             ALU.subtract, ALU.mult))
                for q in range(QT):
                    dve.wait_ge(hi_done, QT * b + q + 1)
                    s.step(dve.tensor_tensor(halves[v][:, q, D:2 * D], xn[:, q, :], halves[v][:, q, 0:D], ALU.subtract))
                assert s.n == YK

            def route_1(c):
                s = Steps(dve, r_step, c, RK)
                dve.wait_ge(logits, c + 1)
                s.link(dve.scalar_tensor_tensor(out=lg, in0=psG, scalar=cR[:, 0:1], in1=bcast(brb, QT),
                                                op0=ALU.mult, op1=ALU.add))
                s.link(dve.tensor_reduce(lm, lg, AX.X, ALU.max))
                s.link(dve.tensor_tensor(lg, lg, spread(lm, E), ALU.subtract))
                dve.wait_ge(e_done, c + 1)
                s.link(dve.tensor_reduce(lsum, ex, AX.X, ALU.add))
                s.link(dve.reciprocal(lr, lsum))
                s.link(dve.tensor_tensor(gt, ex, spread(lr, E), ALU.mult))
                apart(dve, dve_passed)
                for q in range(QT):
                    s.step(dve.max(m8[:, q, :], gt[:, q, :]))
                s.wait()
                apart(dve, dve_passed)
                for q in range(QT):
                    s.step(dve.max_index(ix[:, q, :], m8[:, q, :], gt[:, q, :]))
                s.wait()
                s.link(dve.tensor_copy(ixf, ix[:, :, 0:2].rearrange("p q k -> p k q")))
                s.link(dve.tensor_tensor(oh.rearrange("p k q e -> p (k q) e"), bcast(iota8, 2 * QT),
                                         spread(ixf.rearrange("p k q -> p (k q)"), E), ALU.is_equal))
                s.step(dve.tensor_tensor(mask, oh[:, 0], oh[:, 1], ALU.add))
                assert s.n == R1

            def route_2(c, v, n):
                s = Steps(dve, r_step, c, RK)
                s.n = R1
                dve.wait_ge(counted, c + 1)
                s.link(dve.tensor_copy(base[:, 0, :], count))
                for q in range(1, QT):
                    s.link(dve.tensor_tensor(base[:, q, :], base[:, q - 1, :], psK[:, QT + q - 1, :], ALU.add))
                s.step(dve.tensor_tensor(count, base[:, QT - 1, :], psK[:, 2 * QT - 1, :], ALU.add))
                s.link(dve.tensor_tensor(pos, psK[:, 0:QT, :], base, ALU.add))
                for k in range(2):
                    s.step(dve.tensor_tensor(ohp[:, k], oh[:, k], pos, ALU.mult))
                s.wait()
                s.link(dve.tensor_reduce(pk, ohp, AX.X, ALU.add))
                s.step(dve.tensor_scalar(kp, pk, float(CAP), None, ALU.is_lt))
                s.link(dve.tensor_scalar(away, pk, float(CAP), FAR, ALU.is_ge, ALU.mult))
                s.link(dve.scalar_tensor_tensor(out=dst, in0=ixf, scalar=float(CAP), in1=pk,
                                                op0=ALU.mult, op1=ALU.add))
                dve.wait_ge(row_free[v], n + 1)
                s.step(dve.tensor_tensor(dsti[v], dst, away, ALU.add))
                s.link(dve.tensor_tensor(wk, kp, m8[:, :, 0:2].rearrange("p q k -> p k q"), ALU.mult))
                s.link(dve.tensor_tensor(wsum, wk[:, 0, :], wk[:, 1, :], ALU.add))
                s.link(dve.tensor_scalar(wsum, wsum, 1e-6, None, ALU.max))
                s.link(dve.reciprocal(wi, wsum))
                s.link(dve.tensor_scalar(wi, wi, tf[:, 0:1], None, ALU.mult))
                info = row[v][:, :, D:D + 4]
                s.step(dve.tensor_copy(info[:, :, 0:1].bitcast(U32).rearrange("p q o -> p (q o)"),
                                       tok[:, bass.ds(c * QT, QT)]))
                s.step(dve.tensor_tensor(info[:, :, 1:3], wk.rearrange("p k q -> p q k"), spread(wi, 2), ALU.mult))
                s.step(dve.tensor_copy(info[:, :, 3], ixf[:, 0, :]))
                assert s.n == RK, (s.n, RK)

            dve.wait_ge(w_loaded, 16)
            dve.wait_ge(p_loaded, 80)
            for n in range(4):
                dve.tensor_reduce(mx[:, n:n + 1], W[:, n * KD:(n + 1) * KD, :].rearrange("p c d -> p (c d)"),
                                  AX.X, ALU.max, apply_absolute_value=True).then_inc(mx_done, 1)
            dve.tensor_reduce(mx[:, 4:5], wr.rearrange("p k e -> p (k e)"), AX.X, ALU.max,
                              apply_absolute_value=True).then_inc(mx_done, 1)
            dve.wait_ge(mx_all, 1)
            s = Steps(dve, prep, 0, 40)
            s.link(dve.scalar_tensor_tensor(out=t1[:, 0:1], in0=mx[:, 3:4], scalar=32.0, in1=mx[:, 0:1],
                                            op0=ALU.mult, op1=ALU.add))
            s.link(dve.tensor_scalar(t1[:, 0:1], t1[:, 0:1], 1 / LN_SCALE, TINY, ALU.mult, ALU.max))
            s.link(dve.scalar_tensor_tensor(out=t1[:, 1:2], in0=mx[:, 2:3], scalar=32.0, in1=mx[:, 1:2],
                                            op0=ALU.mult, op1=ALU.max))
            s.link(dve.scalar_tensor_tensor(out=u, in0=t1[:, 1:2], scalar=cinv, in1=t1[:, 0:1],
                                            op0=ALU.mult, op1=ALU.max))
            s.link(dve.tensor_scalar(up2.bitcast(I32), u.bitcast(I32), EXPONENT, None, ALU.bitwise_and))
            s.link(dve.tensor_scalar(sig.bitcast(I32), up2.bitcast(I32), -1, float((254 + TOP) << 23),
                                     ALU.mult, ALU.add))
            s.step(dve.tensor_scalar(sc3[:, 0:1], sig, 1 / LN_SCALE, None, ALU.mult))
            s.step(dve.tensor_scalar(sc3[:, 1:2], sig, cinv, None, ALU.mult))
            s.step(dve.tensor_scalar(sc3[:, 2:3], sig, cinv, 32.0, ALU.mult, ALU.mult))
            s.link(dve.tensor_scalar(t1[:, 0:1], mx[:, 4:5], TINY, None, ALU.max))
            s.link(dve.tensor_scalar(rp2.bitcast(I32), t1[:, 0:1].bitcast(I32), EXPONENT, None, ALU.bitwise_and))
            s.step(dve.tensor_scalar(cR, rp2, 2.0 ** -TOP / LN_SCALE, None, ALU.mult))
            s.link(dve.tensor_scalar(rsc.bitcast(I32), rp2.bitcast(I32), -1, float((254 + TOP) << 23),
                                     ALU.mult, ALU.add))
            s.link(dve.tensor_scalar(wrs[:, :, 0, :], wr, rsc[:, 0:1], None, ALU.mult))
            s.step(dve.scalar_tensor_tensor(out=wrs[:, :, 1, :], in0=wr, scalar=rsc[:, 0:1], in1=wrs[:, :, 0, :],
                                            op0=ALU.mult, op1=ALU.subtract))
            s.link(dve.reciprocal(rw, wtot))
            s.link(dve.tensor_scalar(hcn, hc, rw[:, 0:1], 1 / LN_SCALE, ALU.mult, ALU.mult))
            for k in range(KD):
                s.step(dve.scalar_tensor_tensor(out=W[:, k, :], in0=W[:, 3 * KD + k, :], scalar=hcn[:, k:k + 1],
                                                in1=W[:, k, :], op0=ALU.mult, op1=ALU.add))
            dve.wait_ge(t_done, 2)
            s.step(dve.tensor_scalar(cY, up2, tx[:, 0:1], 2.0 ** -TOP, ALU.mult, ALU.mult))
            s.step(dve.tensor_scalar(bqb, bqb, tx[:, 0:1], None, ALU.mult))
            dve.wait_ge(made, 5)
            s.step(dve.tensor_copy(tri, trif))
            s.step(dve.memset(ones, 1.0))
            s.step(dve.memset(count, 0.0))
            for v in range(2):
                s.step(dve.memset(row[v][:, :, D:D + 4], 0.0))
            ready = s.n
            s.wait()
            for k in range(FT):
                dve.wait_ge(w_hi, k + 1)
                dve.scalar_tensor_tensor(out=Wt[:, k, 1, :], in0=W[:, k, :], scalar=sc3[:, k // KD:k // KD + 1],
                                         in1=Wt[:, k, 0, :], op0=ALU.mult, op1=ALU.subtract).then_inc(w_lo, 1)

            def body(b, v, n, routed=True):
                dve.wait_ge(x_loaded[v], 16 * (n + 1))
                y_part(b, v, 0)
                if routed:
                    route_1(b - 1)
                y_part(b, v, 1)
                norm_part(b, v, n)
                if routed:
                    route_2(b - 1, 1 - v, n if v else n - 1)

            body(0, 0, 0, routed=False)
            body(1, 1, 0)
            with dve.Fori(1, NB // 2) as n:
                body(2 * n, 0, n)
                body(2 * n + 1, 1, n)
            route_1(NB - 1)
            route_2(NB - 1, 1, NB // 2 - 1)

        @block.scalar
        def _(act):
            act.wait_ge(p_loaded, 80)
            act.activation(tx, gx, ACT.Tanh).then_inc(t_done, 1)
            act.activation(tf, gf, ACT.Tanh).then_inc(t_done, 1)
            for k in range(FT):
                if k == 0:
                    act.wait_ge(prep, 17 + KD)
                act.mul(Wt[:, k, 0, :], W[:, k, :], sc3[:, k // KD:k // KD + 1]).then_inc(w_hi, 1)

            def body(b, v, n, routed=True):
                if routed:
                    c = b - 1
                    for q in range(QT):
                        act.wait_ge(turned, QT * c + q + 1)
                        act.copy(xT[:, q].rearrange("p s k i -> p (s k) i"), psR).then_inc(xt_ready, 1)
                    act.wait_ge(r_step, RK * c + 3)
                    act.activation(ex, lg, ACT.Exp).then_inc(e_done, 1)
                act.wait_ge(y_step, YK * b + 4 * QT)
                act.activation(sd, mv[:, :, 1], ACT.Sqrt, bias=lneps[:, 0:1], scale=1 / LN_SCALE ** 2)\
                   .then_inc(sd_done, 1)
                act.wait_ge(row_free[v], n + 1)
                for q in range(QT):
                    act.wait_ge(y_step, YK * b + 4 * QT + 2 + q)
                    act.copy(halves[v][:, q, 0:D], xn[:, q, :]).then_inc(hi_done, 1)

            def tail(c):
                for q in range(QT):
                    act.wait_ge(turned, QT * c + q + 1)
                    act.copy(xT[:, q].rearrange("p s k i -> p (s k) i"), psR).then_inc(xt_ready, 1)
                act.wait_ge(r_step, RK * c + 3)
                act.activation(ex, lg, ACT.Exp).then_inc(e_done, 1)

            act.wait_ge(made, 5)
            body(0, 0, 0, routed=False)
            body(1, 1, 0)
            with act.Fori(1, NB // 2) as n:
                body(2 * n, 0, n)
                body(2 * n + 1, 1, n)
            tail(NB - 1)

        @block.tensor
        def _(pe):
            def merge(b, v, q, first=False):
                if not first:
                    pe.wait_ge(y_step, YK * (b - 1) + 2 * q + 2)
                for k in range(FT):
                    if first:
                        pe.wait_ge(w_lo, k + 1)
                    for s, r in ((0, 0), (0, 1), (1, 0)):
                        mm = pe.matmul(psY[:, q, :], ft[v][:, k // KD, s, k % KD, q * P:(q + 1) * P], Wt[:, k, r, :],
                                       start=(k + s + r == 0), stop=(k == FT - 1 and s == 1))
                mm.then_inc(y_done, 1)

            def router(c, v):
                for q in range(QT):
                    pe.wait_ge(y_step, YK * c + 4 * QT + 2 + QT + q + 1 - 1)
                    if q:
                        pe.wait_ge(xt_ready, QT * c + q)
                    for s in range(2):
                        for k in range(KD):
                            mm = pe.transpose(psR[:, s * KD + k, :], halves[v][:, q, s * D + k * P:s * D + (k + 1) * P],
                                              ident)
                    mm.then_inc(turned, 1)
                for q in range(QT):
                    pe.wait_ge(xt_ready, QT * c + q + 1)
                    for k in range(KD):
                        for s, r in ((0, 0), (0, 1), (1, 0)):
                            mm = pe.matmul(psG[:, q, :], xT[:, q, s, k, :], wrs[:, k, r, :],
                                           start=(k + s + r == 0), stop=(k == KD - 1 and s == 1))
                mm.then_inc(logits, 1)

            def counts(c):
                pe.wait_ge(r_step, RK * c + R1)
                pe.matmul(psK[:, 0:QT, :], tri, mask, start=True, stop=True)
                pe.matmul(psK[:, QT:2 * QT, :], ones, mask, start=True, stop=True).then_inc(counted, 1)

            def body(b, v, n, routed=True):
                pe.wait_ge(f_loaded[v], 16 * (n + 1))
                merge(b, v, 0, first=not routed)
                if routed:
                    router(b - 1, 1 - v)
                merge(b, v, 1, first=not routed)
                if routed:
                    counts(b - 1)

            pe.wait_ge(prep, 24 + KD)
            body(0, 0, 0, routed=False)
            body(1, 1, 0)
            with pe.Fori(1, NB // 2) as n:
                body(2 * n, 0, n)
                body(2 * n + 1, 1, n)
            router(NB - 1, 1)
            counts(NB - 1)


def experts(nc, ps, arena, cst, w1, b1, w2, b2, rows, out):
    E, D, F = w1.shape
    KD, KF = D // P, F // P
    CAP = rows.shape[0] // E
    ST = CAP // P
    HALF = CAP // 2
    ROW = rows.shape[1]
    NT = out.shape[0]
    CH = 8
    take, off = cutter(arena)

    hT = take([KF, 2, CAP], F16)
    XT = take([2, KD, CAP], F16)
    Xr = take([ST, ROW], F32)
    Xh = Xr.bitcast(F16)
    h32 = [take([CAP], F32) for _ in range(2)]
    w1s = take([2, KD * F], F16)
    raw = take([KD * F], F32)
    w2s = take([2, KF * D], F16)
    b2b = take([D], F32)
    o32 = [take([D], F32) for _ in range(2)]
    oa = [take([D], F32) for _ in range(2)]
    b1n, b1T = take([P], F32), take([P], F32)
    mw, mw4, mb = take([1], F32), take([4], F32), take([1], F32)
    wp2, s1, s2, inv1, inv2, hb, hp2, sh = (take([1], F32) for _ in range(8))
    en = take([E], F32)
    eq, da = take([ST], F32), take([ST], F32)
    al, tk = [take([ST], F32) for _ in range(2)], [take([ST], U32) for _ in range(2)]
    ident, identf = cst["ident"], cst["identf"]

    psH = ps[:, 0:4, 0:HALF].rearrange("p (v h) i -> p v h i", h=2)
    psO = ps[:, 4:6, :]
    psX = ps[:, 6, :].bitcast(F16).rearrange("p (c i) -> p c i", i=P)
    psB = ps[:, 7, 0:P]

    with ExitStack() as st:
        def sem(name):
            return st.enter_context(nc.semaphore(name))

        b1_loaded, b1_turned, en_made, init = (sem(s) for s in ("b1_loaded", "b1_turned", "en_made", "init3"))
        raw_loaded = [sem(f"raw_loaded_{c}") for c in range(4)]
        mx_step, mx_all, s_step, s_hi, s_lo = (sem(s) for s in ("wmx_step", "wmx_all", "s_step", "s_hi", "s_lo"))
        x_loaded, x_turned, xt_ready, a_step = (sem(s) for s in ("rows_loaded", "x_turned", "xt3_ready", "a_step"))
        h_done, g_done, h_hi, h_lo = (sem(s) for s in ("h_done", "g_done", "h_hi", "h_lo"))
        o_done, o_bias, o_scaled, added, b2_loaded = (sem(s) for s in (
            "o_done", "o_bias", "o_scaled", "added", "b2_loaded"))
        sp_passed, pool_passed = sem("sp_passed_3"), sem("pool_passed_3")
        block = st.enter_context(nc.Block())
        SK, AK = 6, 7

        @block.sync
        def _(sp):
            def load_w(u, e, second):
                for c in range(4):
                    if second:
                        src = w2[bass.ds(e, 1), c * (F // 4):(c + 1) * (F // 4), :]\
                            .rearrange("o (j p) d -> p (o j) d", p=P)
                        dst = raw.rearrange("p (j d) -> p j d", d=D)[:, c * (KF // 4):(c + 1) * (KF // 4), :]
                    else:
                        src = w1[bass.ds(e, 1), c * P:(c + 1) * P, :].rearrange("o p f -> (o p) f")
                        dst = raw[:, c * F:(c + 1) * F]
                    sp.dma_start(dst, src).then_inc(raw_loaded[c], 16)

            def load_rows(e):
                sp.dma_start(Xr, rows[bass.ds(e * CAP, CAP), :].rearrange("(t p) c -> p t c", p=P))\
                    .then_inc(x_loaded, 16)

            def load_b2(e):
                sp.dma_start(b2b, b2[bass.ds(e, 1), :].partition_broadcast(P).rearrange("p o d -> p (o d)"))\
                    .then_inc(b2_loaded, 16)

            sp.dma_start(b1n, b1.rearrange("e (f p) -> (e f) p", p=P)).then_inc(b1_loaded, 16)
            load_rows(0)
            load_w(0, 0, False)
            load_b2(0)
            sp.wait_ge(s_lo, CH)
            load_w(1, 0, True)
            with sp.Fori(0, E - 1) as e:
                sp.wait_ge(a_step, AK * (e + 1))
                apart(sp, sp_passed)
                sp.wait_ge(x_turned, ST * (e + 1))
                load_rows(e + 1)
                sp.wait_ge(s_lo, CH * (2 * e + 2))
                load_w(2 * e + 2, e + 1, False)
                sp.wait_ge(s_lo, CH * (2 * e + 3))
                load_w(2 * e + 3, e + 1, True)
                sp.wait_ge(o_bias, ST * (e + 1))
                load_b2(e + 1)

        @block.gpsimd
        def _(pool):
            pool.iota(en, pattern=[[1, E]], base=0, channel_multiplier=0,
                      allow_small_or_imprecise_dtypes=True).then_inc(en_made, 1)
            pool.wait_ge(init, 1)
            pool.partition_all_reduce(mb, mb, P, RMAX).then_inc(en_made, 1)

            def reduce_max(u):
                pool.wait_ge(mx_step, 5 * (u + 1))
                apart(pool, pool_passed)
                pool.partition_all_reduce(mw, mw, P, RMAX).then_inc(mx_all, 1)

            def add_rows(e):
                for t in range(ST):
                    pool.wait_ge(o_scaled, ST * e + t + 1)
                    apart(pool, pool_passed)
                    pool.indirect_dma_start(
                        out=out, out_offset=bass.IndirectOffsetOnAxis(ap=tk[1][:, t:t + 1], axis=0),
                        in_=oa[t % 2], in_offset=None, bounds_check=NT - 1, oob_is_err=False,
                        compute_op=ALU.add).then_inc(added, 16)
                    pool.wait_ge(added, 16 * (ST * e + t + 1))
                    if t == 1 and PREP[0]:
                        reduce_max(2 * e + 2)

            PREP = [True]
            reduce_max(0)
            with pool.Fori(0, E - 1) as e:
                reduce_max(2 * e + 1)
                add_rows(e)
            reduce_max(2 * E - 1)
            PREP[0] = False
            add_rows(E - 1)

        @block.vector
        def _(dve):
            def max_part(u, c, second):
                dve.wait_ge(raw_loaded[c], 16 * (u + 1))
                n = KD * F // 4
                s = Steps(dve, mx_step, u, 5)
                s.n = c
                s.step(dve.tensor_reduce(mw4[:, c:c + 1], raw[:, c * n:(c + 1) * n], AX.X, ALU.max,
                                         apply_absolute_value=True))
                if c == 3:
                    s.wait()
                    s.step(dve.tensor_reduce(mw, mw4, AX.X, ALU.max))

            def scales(u, second):
                s = Steps(dve, s_step, u, SK)
                dve.wait_ge(mx_all, u + 1)
                s.link(dve.tensor_scalar(mw, mw, TINY, None, ALU.max))
                s.link(dve.tensor_scalar(wp2.bitcast(I32), mw.bitcast(I32), EXPONENT, None, ALU.bitwise_and))
                if second:
                    s.step(dve.tensor_scalar(s2.bitcast(I32), wp2.bitcast(I32), -1, float((254 + TOP) << 23),
                                             ALU.mult, ALU.add))
                    s.link(dve.tensor_scalar(inv2, wp2, hp2[:, 0:1], 2.0 ** (-2 * TOP), ALU.mult, ALU.mult))
                    s.n += 2
                    dve.sem_inc(s_step, 2)
                else:
                    s.step(dve.tensor_scalar(s1.bitcast(I32), wp2.bitcast(I32), -1, float((254 + TOP) << 23),
                                             ALU.mult, ALU.add))
                    s.link(dve.scalar_tensor_tensor(out=hb, in0=mw, scalar=float(D), in1=mb, op0=ALU.mult,
                                                    op1=ALU.add))
                    s.link(dve.tensor_scalar(hp2.bitcast(I32), hb.bitcast(I32), EXPONENT, None, ALU.bitwise_and))
                    dve.tensor_scalar(inv1, wp2, 2.0 ** -TOP / LN_SCALE, None, ALU.mult)
                    s.link(dve.tensor_scalar(sh.bitcast(I32), hp2.bitcast(I32), -1, float((254 + TOP) << 23),
                                             ALU.mult, ALU.add))

            def low_part(u, c, second):
                n = KD * F // CH
                w, sc = (w2s, s2) if second else (w1s, s1)
                dve.wait_ge(s_hi, CH * u + c + 1)
                dve.scalar_tensor_tensor(out=w[:, 1, c * n:(c + 1) * n], in0=raw[:, c * n:(c + 1) * n],
                                         scalar=sc[:, 0:1], in1=w[:, 0, c * n:(c + 1) * n], op0=ALU.mult,
                                         op1=ALU.subtract).then_inc(s_lo, 1)

            def weights_of(e):
                s = Steps(dve, a_step, e, AK)
                info = Xr[:, :, D:D + 4]
                dve.wait_ge(x_loaded, 16 * e + 16)
                s.step(dve.tensor_copy(tk[0], info[:, :, 0:1].bitcast(U32).rearrange("p t o -> p (t o)")))
                s.step(dve.tensor_scalar(eq, info[:, :, 3], en[:, bass.ds(e, 1)], None, ALU.is_equal))
                s.link(dve.tensor_tensor(da, info[:, :, 1], info[:, :, 2], ALU.subtract))
                s.link(dve.tensor_tensor(da, da, eq, ALU.mult))
                s.link(dve.tensor_tensor(al[0], da, info[:, :, 2], ALU.add))

            def keep_weights(e):
                s = Steps(dve, a_step, e, AK)
                s.n = 5
                s.step(dve.tensor_copy(al[1], al[0]))
                s.step(dve.tensor_copy(tk[1], tk[0]))

            def layer_1(e):
                for f in range(KF):
                    n = e * KF + f
                    if f < 4:
                        max_part(2 * e + 1, f, True)
                    if f == 5:
                        scales(2 * e + 1, True)
                    if 6 <= f < 6 + CH:
                        low_part(2 * e + 1, f - 6, True)
                    dve.wait_ge(h_hi, n + 1)
                    dve.scalar_tensor_tensor(out=hT[:, f, 1, :], in0=h32[f % 2], scalar=sh[:, 0:1],
                                             in1=hT[:, f, 0, :], op0=ALU.mult, op1=ALU.subtract).then_inc(h_lo, 1)

            def layer_2(e, more=True):
                for t in range(ST):
                    n = e * ST + t
                    if t == 0:
                        dve.wait_ge(b2_loaded, 16 * (e + 1))
                    if t >= 2:
                        dve.wait_ge(o_scaled, n - 1)
                    dve.wait_ge(o_done, n + 1)
                    dve.scalar_tensor_tensor(out=o32[t % 2], in0=psO[:, t % 2, :], scalar=inv2[:, 0:1], in1=b2b,
                                             op0=ALU.mult, op1=ALU.add).then_inc(o_bias, 1)
                    if more:
                        if t < 2:
                            max_part(2 * e + 2, 2 * t, False)
                            max_part(2 * e + 2, 2 * t + 1, False)
                        if t == 2:
                            scales(2 * e + 2, False)
                        if t in (2, 3):
                            for c in range(4):
                                low_part(2 * e + 2, 4 * (t - 2) + c, False)

            dve.wait_ge(b1_loaded, 16)
            dve.tensor_reduce(mb, b1n, AX.X, ALU.max, apply_absolute_value=True).then_inc(init, 1)
            dve.wait_ge(b1_turned, 1)
            dve.tensor_copy(b1T, psB).then_inc(init, 1)
            dve.wait_ge(en_made, 2)
            for c in range(4):
                max_part(0, c, False)
            scales(0, False)
            for c in range(CH):
                low_part(0, c, False)
            weights_of(0)
            keep_weights(0)
            with dve.Fori(0, E - 1) as e:
                layer_1(e)
                layer_2(e)
                weights_of(e + 1)
                dve.wait_ge(added, 16 * ST * (e + 1))
                keep_weights(e + 1)
            layer_1(E - 1)
            layer_2(E - 1, more=False)

        @block.scalar
        def _(act):
            def high_part(u, c, second):
                n = KD * F // CH
                w, sc = (w2s, s2) if second else (w1s, s1)
                if c == 0:
                    act.wait_ge(s_step, SK * u + 3)
                act.mul(w[:, 0, c * n:(c + 1) * n], raw[:, c * n:(c + 1) * n], sc[:, 0:1]).then_inc(s_hi, 1)

            def turned(e, t):
                act.wait_ge(x_turned, ST * e + t + 1)
                act.copy(XT[:, :, :, t * P:(t + 1) * P], psX.rearrange("p (s k) i -> p s k i", s=2))\
                   .then_inc(xt_ready, 1)

            def layer_1(e):
                for f in range(KF):
                    n = e * KF + f
                    act.wait_ge(h_done, n + 1)
                    if f == 0:
                        act.wait_ge(s_step, SK * (2 * e + 1))
                    if f >= 2:
                        act.wait_ge(h_lo, n - 1)
                    act.activation(h32[f % 2].rearrange("p (h i) -> p h i", h=2), psH[:, f % 2], ACT.Gelu,
                                   bias=b1T[:, bass.ds(n, 1)], scale=inv1[:, 0:1]).then_inc(g_done, 1)
                    act.wait_ge(g_done, n + 1)
                    act.mul(hT[:, f, 0, :], h32[f % 2], sh[:, 0:1]).then_inc(h_hi, 1)
                    if 5 <= f < 5 + CH:
                        high_part(2 * e + 1, f - 5, True)

            def layer_2(e, more=True):
                for t in range(ST):
                    n = e * ST + t
                    if more:
                        turned(e + 1, t)
                        if t in (2, 3):
                            for c in range(4):
                                high_part(2 * e + 2, 4 * (t - 2) + c, False)
                    act.wait_ge(o_bias, n + 1)
                    if t >= 2:
                        act.wait_ge(added, 16 * (n - 1))
                    act.mul(oa[t % 2], o32[t % 2], al[1][:, t:t + 1]).then_inc(o_scaled, 1)

            act.wait_ge(init, 2)
            for t in range(ST):
                turned(0, t)
            for c in range(CH):
                high_part(0, c, False)
            with act.Fori(0, E - 1) as e:
                layer_1(e)
                layer_2(e)
            layer_1(E - 1)
            layer_2(E - 1, more=False)

        @block.tensor
        def _(pe):
            def turn(e, t):
                if t:
                    pe.wait_ge(xt_ready, ST * e + t)
                else:
                    pe.wait_ge(x_loaded, 16 * (e + 1))
                for s in range(2):
                    for k in range(KD):
                        mm = pe.transpose(psX[:, s * KD + k, :], Xh[:, t, s * D + k * P:s * D + (k + 1) * P], ident)
                mm.then_inc(x_turned, 1)

            def layer_1(e):
                pe.wait_ge(xt_ready, ST * (e + 1))
                pe.wait_ge(s_lo, CH * (2 * e + 1))
                for f in range(KF):
                    n = e * KF + f
                    if f >= 2:
                        pe.wait_ge(g_done, n - 1)
                    for k in range(KD):
                        for s, r in ((0, 0), (0, 1), (1, 0)):
                            for h in range(2):
                                mm = pe.matmul(psH[:, f % 2, h, :], w1s[:, s, k * F + f * P:k * F + (f + 1) * P],
                                               XT[:, r, k, h * HALF:(h + 1) * HALF],
                                               start=(k + s + r == 0), stop=(k == KD - 1 and s == 1))
                    mm.then_inc(h_done, 1)

            def layer_2(e, more=True):
                pe.wait_ge(s_lo, CH * (2 * e + 2))
                for t in range(ST):
                    n = e * ST + t
                    if more:
                        turn(e + 1, t)
                    if t >= 2:
                        pe.wait_ge(o_bias, n - 1)
                    for f in range(KF):
                        if t == 0:
                            pe.wait_ge(h_lo, e * KF + f + 1)
                        for s, r in ((0, 0), (0, 1), (1, 0)):
                            mm = pe.matmul(psO[:, t % 2, :], hT[:, f, s, t * P:(t + 1) * P],
                                           w2s[:, r, f * D:(f + 1) * D],
                                           start=(f + s + r == 0), stop=(f == KF - 1 and s == 1))
                    mm.then_inc(o_done, 1)

            pe.wait_ge(b1_loaded, 16)
            pe.transpose(psB, b1n, identf).then_inc(b1_turned, 1)
            for t in range(ST):
                turn(0, t)
            with pe.Fori(0, E - 1) as e:
                layer_1(e)
                layer_2(e)
            layer_1(E - 1)
            layer_2(E - 1, more=False)


def gated_layer(nc, x, ctx, g_x, g_f, w_sim, b_sim, w_qv, b_qv, w_r, b_r, w1, b1, w2, b2, out):
    x, ctx, out = (a.rearrange("o n d -> (o n) d") for a in (x, ctx, out))
    NI, D = x.shape
    E = w_r.shape[1]
    CAP = max(1, int(1.25 * NI / E))
    ROW = D + 4
    with ExitStack() as st:
        def sbuf(name, shape, dtype):
            return st.enter_context(nc.sbuf_tensor(name, shape, dtype))[:]

        arena = sbuf("arena", [P, 52400], F32)
        cst = {"ident": sbuf("ident", [P, P], F16), "identf": sbuf("identf", [P, P], F32),
               "onesf": sbuf("onesf", [P, P], F32)}
        pooled = sbuf("pooled", [P, 8], F32)
        hc = {"hc": pooled[:, 0:4], "wtot": pooled[:, 4:5], "ctx_inv": pooled[:, 5:6], "ctx_scale": pooled[:, 6:7]}
        ps = st.enter_context(nc.psum_tensor("ps", [P, 8, 512], F32))
        feats = nc.dram_tensor("feats", [NI // 256, P, 3, 2048], F16, kind="Internal").ap()
        rows = nc.dram_tensor("rows", [E * CAP, ROW], F32, kind="Internal").ap()
        attention(nc, ps, arena, cst, x, ctx, w_sim, b_sim, feats, rows, hc)
        merge_and_route(nc, ps, arena, cst, x, w_qv, b_qv, g_x, g_f, w_r, b_r, feats, rows, out, hc)
        experts(nc, ps, arena, cst, w1, b1, w2, b2, rows, out)


_INS = ['x', 'ctx_1024', 'g_xattn', 'g_ffn', 'L0_xattn_w_sim', 'L0_xattn_b_sim', 'L0_xattn_W_qv', 'L0_xattn_b_qv',
        'L0_ffn_w_router', 'L0_ffn_b_router', 'L0_ffn_w1', 'L0_ffn_b1', 'L0_ffn_w2', 'L0_ffn_b2']


def kernel(**inputs):
    import numpy as np
    import concourse.bacc as bacc
    from concourse.bass_utils import run_bass_kernel_spmd

    nc = bacc.Bacc("TRN2", target_bir_lowering=False, num_devices=1)
    arrays, args = {}, []
    for name in _INS:
        a = np.ascontiguousarray(inputs[name])
        arrays[f"in_{name}"] = a
        args.append(nc.dram_tensor(f"in_{name}", a.shape, mybir.dt.from_np(a.dtype), kind="ExternalInput").ap())
    out = nc.dram_tensor("out", inputs["x"].shape, F32, kind="ExternalOutput").ap()
    gated_layer(nc, *args, out)
    r = run_bass_kernel_spmd(nc, [arrays], core_ids=[0])
    return r.results[0]["out"]
```

```python
from contextlib import ExitStack

import concourse.bass as bass
from concourse import mybir

ALU = mybir.AluOpType
ACT = mybir.ActivationFunctionType
F32 = mybir.dt.float32
F16 = mybir.dt.float16
I32 = mybir.dt.int32
U32 = mybir.dt.uint32
AX = mybir.AxisListType
RMAX = bass.bass_isa.ReduceOp.max

P = 128
TOP = 14
EXPONENT = 0x7F800000
TINY = 2.0 ** -100
LN_SCALE = 2.0 ** 10
P_SCALE = 2.0 ** 15
LN_EPS = 1e-5
EARLY = 30000
NEVER = -1e30


class Steps:

    def __init__(self, eng, sem, call, per, start=0):
        self.eng, self.sem, self.per, self.n = eng, sem, per, 0
        self.base = call * per + start

    def step(self, instruction):
        instruction.then_inc(self.sem, 1)
        self.n += 1
        assert self.n <= self.per

    def wait(self):
        self.eng.wait_ge(self.sem, self.base + self.n)

    def link(self, instruction):
        self.step(instruction)
        self.wait()


def apart(eng, passed):
    eng.sem_inc(passed, 1)


def bcast(ap, n):
    return ap[:, None, :].broadcast_to([ap.shape[0], n, ap.shape[1]])


def spread(ap, n):
    return ap[:, :, None].broadcast_to([ap.shape[0], ap.shape[1], n])


def cutter(arena):
    off = [0]

    def take(shape, dtype, at=None):
        n = 1
        for s in shape:
            n *= s
        words = n * (2 if dtype == F16 else 4) // 4
        a = off[0] if at is None else at
        if at is None:
            off[0] += words
        assert a + words <= arena.shape[1], (a + words, arena.shape)
        v = arena[:, a:a + words]
        if dtype != F32:
            v = v.bitcast(dtype)
        names = "abcdef"[:len(shape)]
        if len(shape) > 1:
            v = v.rearrange(f"p ({' '.join(names)}) -> p {' '.join(names)}",
                            **{names[i]: shape[i] for i in range(1, len(shape))})
        return v

    return take, off


class ExpertWeights:
    CH = 8
    SK = 6

    def __init__(self, nc, st, arena, at, w1, b1, w2):
        def sem(name):
            return st.enter_context(nc.semaphore(name))

        self.w1, self.b1, self.w2 = w1, b1, w2
        self.E, self.D, self.F = E, D, F = w1.shape
        self.KD, self.KF = D // P, F // P
        take, _ = cutter(arena[:, at:])
        self.w1s = take([2, self.KD * F], F16)
        self.w2s = None
        self.raw = take([self.KD * F], F32)
        self.b1n, self.b1T = take([P], F32), take([P], F32)
        self.mw, self.mw4, self.mb = take([1], F32), take([4], F32), take([1], F32)
        self.wp2, self.s1, self.s2, self.inv1, self.inv2, self.hb, self.hp2, self.sh = (
            take([1], F32) for _ in range(8))
        self.en = take([E], F32)
        self.b1_loaded, self.b1_turned, self.en_made, self.init = (
            sem(s) for s in ("b1_loaded", "b1_turned", "en_made", "init3"))
        self.raw_loaded = [sem(f"raw_loaded_{c}") for c in range(4)]
        self.mx_step, self.mx_all, self.s_step, self.s_hi, self.s_lo = (
            sem(s) for s in ("wmx_step", "wmx_all", "s_step", "s_hi", "s_lo"))
        self.pool_passed = sem("pool_passed_w")

    def load(self, sp, e, second):
        D, F, KF = self.D, self.F, self.KF
        for c in range(4):
            if second:
                src = self.w2[bass.ds(e, 1), c * (F // 4):(c + 1) * (F // 4), :]\
                    .rearrange("o (j p) d -> p (o j) d", p=P)
                dst = self.raw.rearrange("p (j d) -> p j d", d=D)[:, c * (KF // 4):(c + 1) * (KF // 4), :]
            else:
                src = self.w1[bass.ds(e, 1), c * P:(c + 1) * P, :].rearrange("o p f -> (o p) f")
                dst = self.raw[:, c * F:(c + 1) * F]
            sp.dma_start(dst, src).then_inc(self.raw_loaded[c], 16)

    def reduce_max(self, pool, u):
        pool.wait_ge(self.mx_step, 5 * (u + 1))
        apart(pool, self.pool_passed)
        pool.partition_all_reduce(self.mw, self.mw, P, RMAX).then_inc(self.mx_all, 1)

    def max_part(self, dve, u, c):
        dve.wait_ge(self.raw_loaded[c], 16 * (u + 1))
        n = self.KD * self.F // 4
        s = Steps(dve, self.mx_step, u, 5)
        s.n = c
        s.step(dve.tensor_reduce(self.mw4[:, c:c + 1], self.raw[:, c * n:(c + 1) * n], AX.X, ALU.max,
                                 apply_absolute_value=True))
        if c == 3:
            s.wait()
            s.step(dve.tensor_reduce(self.mw, self.mw4, AX.X, ALU.max))

    def scales(self, dve, u, second):
        s = Steps(dve, self.s_step, u, self.SK)
        mw, wp2, hp2, hb = self.mw, self.wp2, self.hp2, self.hb
        dve.wait_ge(self.mx_all, u + 1)
        s.link(dve.tensor_scalar(mw, mw, TINY, None, ALU.max))
        s.link(dve.tensor_scalar(wp2.bitcast(I32), mw.bitcast(I32), EXPONENT, None, ALU.bitwise_and))
        if second:
            s.step(dve.tensor_scalar(self.s2.bitcast(I32), wp2.bitcast(I32), -1, float((254 + TOP) << 23),
                                     ALU.mult, ALU.add))
            s.link(dve.tensor_scalar(self.inv2, wp2, hp2[:, 0:1], 2.0 ** (-2 * TOP), ALU.mult, ALU.mult))
            s.n += 2
            dve.sem_inc(self.s_step, 2)
        else:
            s.step(dve.tensor_scalar(self.s1.bitcast(I32), wp2.bitcast(I32), -1, float((254 + TOP) << 23),
                                     ALU.mult, ALU.add))
            s.link(dve.scalar_tensor_tensor(out=hb, in0=mw, scalar=float(self.D), in1=self.mb, op0=ALU.mult,
                                            op1=ALU.add))
            s.link(dve.tensor_scalar(hp2.bitcast(I32), hb.bitcast(I32), EXPONENT, None, ALU.bitwise_and))
            dve.tensor_scalar(self.inv1, wp2, 2.0 ** -TOP / LN_SCALE, None, ALU.mult)
            s.link(dve.tensor_scalar(self.sh.bitcast(I32), hp2.bitcast(I32), -1, float((254 + TOP) << 23),
                                     ALU.mult, ALU.add))

    def split(self, second):
        return (self.w2s, self.s2) if second else (self.w1s, self.s1)

    def high_part(self, act, u, c, second):
        n = self.KD * self.F // self.CH
        w, sc = self.split(second)
        if c == 0:
            act.wait_ge(self.s_step, self.SK * u + 3)
        act.mul(w[:, 0, c * n:(c + 1) * n], self.raw[:, c * n:(c + 1) * n], sc[:, 0:1]).then_inc(self.s_hi, 1)

    def low_part(self, dve, u, c, second):
        n = self.KD * self.F // self.CH
        w, sc = self.split(second)
        dve.wait_ge(self.s_hi, self.CH * u + c + 1)
        dve.scalar_tensor_tensor(out=w[:, 1, c * n:(c + 1) * n], in0=self.raw[:, c * n:(c + 1) * n],
                                 scalar=sc[:, 0:1], in1=w[:, 0, c * n:(c + 1) * n], op0=ALU.mult,
                                 op1=ALU.subtract).then_inc(self.s_lo, 1)


def attention(nc, ps, arena, cst, x, ctx, w_sim, b_sim, feats, rows, hc_out):
    D = x.shape[1]
    KD = D // P
    NI, J = x.shape[0], ctx.shape[0]
    IB = 256
    NB = NI // IB
    QT = IB // P
    JT = -(-J // P)
    NP = JT // 2
    JR = J - (JT - 1) * P
    AHEAD = 5
    SLOTS = NP + AHEAD
    assert JT == 2 * NP

    take, off = cutter(arena)

    ctxT = take([2, KD, JT * P], F16)
    S = take([SLOTS, 2, IB], F32)
    at = off[0]
    ctxN = take([JT, 2, D], F16)
    raw = take([JT, D], F32, at)
    eT = take([2, 2, KD, IB], F16)
    qT = take([2, KD, IB], F16)
    prob = take([3, 2, 2, IB], F16)
    M = take([2, IB], F32)
    Mc = take([IB], F32)
    Mb = take([2, IB], F32)
    L = take([2, IB], F32)
    R = take([IB], F32)
    wrow = take([IB], F32)
    dg = take([2, QT, P], F32)
    xs = take([QT, D], F32)
    eh = take([QT, 2, D], F16)
    es = take([KD, P], F32)
    ehs = take([2, IB], F32)
    at = off[0]
    hq = take([KD, IB], F32)
    ch = take([2, 2, D], F16, at)
    feat = take([2, 2, KD, IB], F16)
    e32 = take([KD, IB], F32)
    w1b = take([D], F32)
    wcol = take([2, KD], F32)
    wq = take([2, KD], F32)
    wmx = take([2], F32)
    bound, qp2, qscale = take([1], F32), take([1], F32), take([1], F32)
    ew, ewt = take([NI // P], F32), take([QT], F32)
    cmax = take([JT], F32)
    gmax, gp2, gscale, sinv = (take([1], F32) for _ in range(4))
    pad, zero = take([1], F32), take([1], F32)
    bs = take([1], F32)
    stats, mv, sd, rs = take([QT, 6], F32), take([QT, 2], F32), take([QT], F32), take([QT], F32)
    m2 = take([2, QT], F32)
    top, new, neg, rr, ws = (take([1], F32) for _ in range(5))
    hcp = take([KD], F32)
    lneps = take([1], F32)
    blank = take([rows.shape[1]], F32)
    ident, identf, onesf = cst["ident"], cst["identf"], cst["onesf"]
    hc, wtot, cinv_g, cscale_g = hc_out["hc"], hc_out["wtot"], hc_out["ctx_inv"], hc_out["ctx_scale"]

    psS = ps[:, 0:2, :].rearrange("p s (h i) -> p s h i", h=2)
    psA = ps[:, 2:6, 0:IB]
    psT = [ps[:, 2 + h, :].bitcast(F16).rearrange("p (c i) -> p c i", i=P) for h in range(2)]
    psE = ps[:, 6, :].bitcast(F16).rearrange("p (c i) -> p c i", i=P)
    psL = ps[:, 6, 0:IB]
    psC = ps[:, 7, :]

    with ExitStack() as st:
        def sem(name):
            return st.enter_context(nc.semaphore(name))

        const_loaded, made, tail_zero, tail_loaded, setup = (sem(s) for s in (
            "const_loaded", "made", "tail_zero", "tail_loaded", "setup"))
        GROUPS = 5
        GT = (JT - 1) // GROUPS
        assert GT * GROUPS == JT - 1
        ctx_loaded = [sem(f"ctx_loaded_{g}") for g in range(GROUPS)]
        g_step, g_all, q_all = (sem(s) for s in ("g_step", "g_all", "q_all"))
        c_hi, c_lo, c_kept, ct_done, ct_act, ct_dve = (sem(s) for s in (
            "c_hi", "c_lo", "c_kept", "ct_done", "ct_act", "ct_dve"))
        x_loaded, ln_step, ln_sd, ln_hi, ln_t, et_ready, et_out, q_step, q_hi = (sem(s) for s in (
            "x_loaded", "ln_step", "ln_sd", "ln_hi", "ln_t", "et_ready", "et_out", "q_step", "q_hi"))
        qk_done, scores_ready, max_done, sub_done, exp_done, hi_done, p_ready, slot_free, av_done = (
            sem(s) for s in ("qk_done", "scores_ready", "max_done", "sub_done", "exp_done",
                             "hi_done", "p_ready", "slot_free", "av_done"))
        merge_done, mT_done, dg_step, mb_done, mb_ready, lsum_done, acc_step = (sem(s) for s in (
            "merge_done", "mT_done", "dg_step", "mb_done", "mb_ready", "lsum_done", "acc_step"))
        rows_blank = sem("rows_blank")
        f_hi, f_eh, f_lo, f_out = (sem(s) for s in ("f_hi", "f_eh", "f_lo", "f_out"))
        hc_step, hc_w, e_step = (sem(s) for s in ("hc_step", "hc_w", "e_step"))
        sp_passed, dve_passed = sem("sp_passed"), sem("dve_passed")
        block = st.enter_context(nc.Block())
        LK = 5 * QT + 2
        QK = QT * (KD + 2)
        ACK, HK, EK, DK = KD + 1, 5, 2 * KD, 2 * QT + 2

        @block.sync
        def _(sp):
            def load_x(b):
                sp.dma_start(xs, x[bass.ds(b * IB, IB), :].rearrange("(q p) d -> p q d", p=P))\
                    .then_inc(x_loaded, 16)

            def store_e(b):
                sp.wait_ge(et_ready, QT * b + QT)
                sp.dma_start(feats[bass.ds(b, 1), :, 0, :].rearrange("o p c -> (o p) c"),
                             eT[:, bass.ds(b % 2, 1)].rearrange("p o s k i -> p (o s k i)"))\
                    .then_inc(et_out, 16)
                sp.wait_ge(et_out, 16 * b + 16)

            def store_f(c):
                sp.wait_ge(f_lo, KD * c + KD)
                sp.dma_start(feats[bass.ds(c, 1), :, 1:3, :].rearrange("o p f c -> (o p) (f c)"),
                             feat.rearrange("p f s k i -> p (f s k i)")).then_inc(f_out, 16)
                sp.wait_ge(f_out, 16 * c + 32)
                apart(sp, sp_passed)

            sp.sem_inc(f_out, 16)
            load_x(0)
            for g in range(GROUPS):
                sp.dma_start(raw[:, g * GT:(g + 1) * GT, :],
                             ctx[g * GT * P:(g + 1) * GT * P, :].rearrange("(j p) d -> p j d", p=P))\
                    .then_inc(ctx_loaded[g], 16)
                if g == 0:
                    with nc.allow_non_contiguous_dma("two columns of w_sim, once"):
                        for n in (1, 2):
                            sp.dma_start(wcol[:, n - 1, :], w_sim[n * D:(n + 1) * D].rearrange("(k p) -> p k", p=P))\
                                .then_inc(const_loaded, 16)
                    sp.dma_start(w1b, w_sim[0:D].partition_broadcast(P)).then_inc(const_loaded, 16)
                    sp.dma_start(bs, b_sim.partition_broadcast(P)).then_inc(const_loaded, 16)
            sp.wait_ge(tail_zero, 1)
            sp.dma_start(raw[0:JR, JT - 1, :], ctx[(JT - 1) * P:J, :]).then_inc(tail_loaded, 16)
            sp.wait_ge(made, 9)
            sp.dma_start(rows.rearrange("(t p) c -> p t c", p=P), bcast(blank, rows.shape[0] // P))\
                .then_inc(rows_blank, 16)
            for b in range(2):
                sp.wait_ge(ln_step, LK * (b + 1))
                load_x(b + 1)
                store_e(b)
            with sp.Fori(2, NB - 1) as b:
                sp.wait_ge(ln_step, LK * (b + 1))
                load_x(b + 1)
                store_e(b)
                store_f(b - 2)
            store_f(NB - 3)
            store_e(NB - 1)
            store_f(NB - 2)
            store_f(NB - 1)
            sp.wait_ge(rows_blank, 16)

        @block.gpsimd
        def _(pool):
            pool.memset(raw[:, JT - 1, :], 0.0).then_inc(tail_zero, 1)
            pool.memset(onesf, 1.0).then_inc(made, 1)
            pool.memset(identf, 0.0).then_inc(made, 1)
            pool.memset(pad, NEVER).then_inc(made, 1)
            pool.memset(zero, 0.0).then_inc(made, 1)
            pool.memset(lneps, LN_EPS / LN_SCALE ** 2).then_inc(made, 1)
            pool.memset(blank, 0.0).then_inc(made, 1)
            pool.wait_ge(made, 6)
            pool.iota(blank[:, D:D + 1].bitcast(U32), pattern=[[0, 1]], base=NI, channel_multiplier=0)\
                .then_inc(made, 1)
            pool.memset(pad[0:JR, :], 0.0).then_inc(made, 1)
            pool.affine_select(out=identf, in_=identf, compare_op=ALU.not_equal, fill=1.0, base=0,
                               pattern=[[-1, P]], channel_multiplier=1).then_inc(made, 1)
            pool.wait_ge(setup, 5)
            pool.partition_all_reduce(wmx, wmx, P, RMAX).then_inc(q_all, 1)
            pool.wait_ge(g_step, 1)
            pool.partition_all_reduce(gmax, gmax, P, RMAX).then_inc(g_all, 1)

        @block.vector
        def _(dve):
            def norm_stats(b):
                s = Steps(dve, ln_step, b, LK)
                dve.wait_ge(x_loaded, 16 * b + 16)
                for q in range(QT):
                    s.step(dve.bn_stats(stats[:, q, :], xs[:, q, :]))
                s.wait()
                apart(dve, dve_passed)
                for q in range(QT):
                    s.step(dve.bn_aggr(mv[:, q, :], stats[:, q, :]))

            def norm(b):
                s = Steps(dve, ln_step, b, LK)
                s.n = 2 * QT
                dve.wait_ge(ln_sd, b + 1)
                s.link(dve.reciprocal(rs, sd))
                for q in range(QT):
                    s.step(dve.tensor_scalar(xs[:, q, :], xs[:, q, :], mv[:, q, 0:1], rs[:, q:q + 1],
                                             ALU.subtract, ALU.mult))

            def norm_lo(b):
                s = Steps(dve, ln_step, b, LK)
                s.n = 3 * QT + 1
                for q in range(QT):
                    dve.wait_ge(ln_hi, QT * b + q + 1)
                    s.step(dve.tensor_tensor(eh[:, q, 1, :], xs[:, q, :], eh[:, q, 0, :], ALU.subtract))
                for q in range(QT):
                    s.step(dve.tensor_tensor_reduce(out=xs[:, q, :], in0=xs[:, q, :], in1=w1b,
                                                    scale=1 / LN_SCALE, scalar=bs[:, 0:1], op0=ALU.mult,
                                                    op1=ALU.add, accum_out=ewt[:, q:q + 1]))
                s.wait()
                s.step(dve.tensor_copy(ew[:, bass.ds(b * QT, QT)], ewt))

            def query(b, q):
                s = Steps(dve, q_step, b, QK)
                s.n = q * (KD + 2)
                et = eT[:, bass.ds(b % 2, 1)].rearrange("p o s k i -> p (o s) k i")[:, :, :, q * P:(q + 1) * P]
                dve.wait_ge(et_ready, QT * b + q + 1)
                if q:
                    s.wait()
                s.link(dve.tensor_tensor(es, et[:, 0], et[:, 1], ALU.add))
                for k in range(KD):
                    s.step(dve.tensor_scalar(es[:, k, :], es[:, k, :], wq[:, 1, k:k + 1], wq[:, 0, k:k + 1],
                                             ALU.mult, ALU.add))

            def query_lo(b, q):
                s = Steps(dve, q_step, b, QK)
                s.n = q * (KD + 2) + KD + 1
                dve.wait_ge(q_hi, QT * b + q + 1)
                s.step(dve.tensor_tensor(qT[:, 1, :, q * P:(q + 1) * P], es, qT[:, 0, :, q * P:(q + 1) * P],
                                         ALU.subtract))

            def scale_of(s, sc, p2, m):
                s.link(dve.tensor_scalar(p2.bitcast(I32), m.bitcast(I32), EXPONENT, None, ALU.bitwise_and))
                s.link(dve.tensor_scalar(sc.bitcast(I32), p2.bitcast(I32), -1, float((254 + TOP) << 23),
                                         ALU.mult, ALU.add))

            def running_max(b, t):
                n = b * NP + t
                dve.wait_ge(scores_ready, n + 3)
                if t == 0:
                    dve.tensor_copy(M, slot_of(n)).then_inc(max_done, 1)
                else:
                    dve.wait_ge(max_done, n)
                    dve.tensor_tensor(M, M, slot_of(n), ALU.max).then_inc(max_done, 1)

            def slot_of(a):
                return S[:, bass.ds(a % SLOTS, 1)].rearrange("p o h i -> p (o h) i")

            def split_pair(t):
                for h in range(2):
                    j = 2 * t + h
                    dve.wait_ge(c_hi, j + 1)
                    dve.scalar_tensor_tensor(out=ch[:, h, 1, :], in0=raw[:, j, :], scalar=gscale[:, 0:1],
                                             in1=ch[:, h, 0, :], op0=ALU.mult, op1=ALU.subtract)\
                       .then_inc(c_lo, 1)
                for h in range(2):
                    j = 2 * t + h
                    dve.wait_ge(c_lo, j + 1)
                    dve.tensor_copy(ctxN[:, j], ch[:, h]).then_inc(c_kept, 1)
                dve.wait_ge(ct_done, 2 * t + 4)
                dve.tensor_copy(ctxT[:, :, :, (2 * t + 1) * P:(2 * t + 2) * P],
                                psT[1].rearrange("p (s k) i -> p s k i", s=2)).then_inc(ct_dve, 1)

            def subtract(a):
                dve.tensor_tensor(slot_of(a), slot_of(a), bcast(Mb[:, 0, :], 2), ALU.subtract)\
                   .then_inc(sub_done, 1)

            def low_and_sum(a, first):
                dve.wait_ge(hi_done, a + 1)
                pr = prob[:, bass.ds(a % 3, 1)].rearrange("p o s h i -> p (o s) h i")
                dve.scalar_tensor_tensor(out=pr[:, 1], in0=slot_of(a), scalar=P_SCALE, in1=pr[:, 0],
                                         op0=ALU.mult, op1=ALU.subtract).then_inc(p_ready, 1)
                if first:
                    dve.tensor_copy(L, slot_of(a)).then_inc(slot_free, 1)
                else:
                    dve.wait_ge(slot_free, SLOTS + a)
                    dve.tensor_tensor(L, L, slot_of(a), ALU.add).then_inc(slot_free, 1)

            def merge_maxima(c):
                dve.wait_ge(max_done, NP * (c + 1))
                dve.tensor_tensor(Mc, M[:, 0, :], M[:, 1, :], ALU.max).then_inc(merge_done, 1)

            def maxima(c):
                dve.wait_ge(mT_done, c + 1)
                s = Steps(dve, dg_step, c, DK)
                s.link(dve.tensor_reduce(m2[:, 0, :], psC[:, 0:IB].rearrange("p (q i) -> p q i", q=QT),
                                         AX.X, ALU.max))
                s.link(dve.tensor_tensor(m2[:, 1, :], m2[:, 0, :], ew[:, bass.ds(c * QT, QT)], ALU.add))
                for n in range(2):
                    for q in range(QT):
                        s.step(dve.tensor_scalar(dg[:, n, q, :], identf, m2[:, n, q:q + 1], None, ALU.mult))

            def take_acc(c):
                s = Steps(dve, acc_step, c, ACK)
                dve.wait_ge(lsum_done, c + 1)
                s.link(dve.reciprocal(R, psL))
                dve.wait_ge(av_done, NP * (c + 1) + 3)
                for k in range(KD):
                    s.step(dve.scalar_tensor_tensor(out=hq[:, k, :], in0=psA[:, k, :], scalar=1 / P_SCALE,
                                                    in1=R, op0=ALU.mult, op1=ALU.mult))

            def products(c, k):
                dve.wait_ge(acc_step, ACK * (c + 1))
                dve.wait_ge(e_step, EK * (c + 1))
                if k >= 2:
                    dve.wait_ge(f_lo, KD * c + k - 1)
                dve.scalar_tensor_tensor(out=ehs[:, k % 2, :], in0=hq[:, k, :], scalar=1 / LN_SCALE / 32,
                                         in1=e32[:, k, :], op0=ALU.mult, op1=ALU.mult).then_inc(f_eh, 1)

            def lows(c, k):
                n = KD * c + k
                dve.wait_ge(f_hi, 2 * n + 1)
                dve.tensor_tensor(feat[:, 0, 1, k, :], hq[:, k, :], feat[:, 0, 0, k, :], ALU.subtract)
                dve.wait_ge(f_hi, 2 * n + 2)
                dve.tensor_tensor(feat[:, 1, 1, k, :], ehs[:, k % 2, :], feat[:, 1, 0, k, :], ALU.subtract)\
                   .then_inc(f_lo, 1)

            def pool_top(c):
                s = Steps(dve, hc_step, c, HK)
                s.link(dve.tensor_reduce(new, Mb[:, 1, :], AX.X, ALU.max))
                s.link(dve.tensor_tensor(new, new, top, ALU.max))
                s.step(dve.tensor_scalar(neg, new, -1.0, None, ALU.mult))

            def pool_part(c, k):
                s = Steps(dve, e_step, c, EK)
                s.n = 2 * k
                et = eT[:, bass.ds(c % 2, 1)].rearrange("p o s k i -> p (o s) k i")
                if k:
                    s.wait()
                s.link(dve.tensor_tensor(e32[:, k, :], et[:, 0, k, :], et[:, 1, k, :], ALU.add))
                if k == 0:
                    dve.wait_ge(hc_w, 2 * c + 2)
                s.step(dve.tensor_tensor_reduce(out=Mc, in0=e32[:, k, :], in1=wrow, scale=1.0, scalar=0.0,
                                                op0=ALU.mult, op1=ALU.add, accum_out=hcp[:, k:k + 1]))

            def pool_update(c):
                s = Steps(dve, hc_step, c, HK)
                s.n = 3
                dve.wait_ge(e_step, EK * (c + 1))
                dve.tensor_copy(top, new)
                s.step(dve.scalar_tensor_tensor(out=hc, in0=hc, scalar=rr[:, 0:1], in1=hcp,
                                                op0=ALU.mult, op1=ALU.add))
                s.link(dve.scalar_tensor_tensor(out=wtot, in0=wtot, scalar=rr[:, 0:1], in1=ws,
                                                op0=ALU.mult, op1=ALU.add))

            def iteration(b, first=False, last=False, norms=True):
                if first:
                    merge_maxima(0)
                    maxima(0)
                else:
                    take_acc(b - 2)
                dve.wait_ge(mb_ready, b)
                a0 = NP * (b - 1)
                subtract(a0)
                if not last:
                    running_max(b, 0)
                subtract(a0 + 1)
                subtract(a0 + 2)
                if not last:
                    running_max(b, 1)
                low_and_sum(a0, True)
                pool_top(b - 1)
                if not last:
                    for t in range(2, AHEAD):
                        running_max(b, t)
                for t in range(NP):
                    if t + 1 < NP:
                        low_and_sum(a0 + t + 1, False)
                    if t + 3 < NP:
                        subtract(a0 + t + 3)
                    if not first and t < KD:
                        products(b - 2, t)
                    if not first and 1 <= t <= KD:
                        lows(b - 2, t - 1)
                    if 1 <= t <= KD:
                        pool_part(b - 1, t - 1)
                    if t == KD + 1:
                        pool_update(b - 1)
                    if norms:
                        if t == 0:
                            norm_stats(b + 1)
                        if t == 2:
                            norm(b + 1)
                        if t == 4:
                            norm_lo(b + 1)
                    if not last:
                        if t == 8:
                            merge_maxima(b)
                        if t == 10:
                            maxima(b)
                    if norms:
                        if t in (8, 11):
                            query(b + 1, (t - 8) // 3)
                        if t in (10, 12):
                            query_lo(b + 1, (t - 10) // 2)
                    if not last and t + AHEAD < NP:
                        running_max(b, t + AHEAD)

            dve.sem_inc(slot_free, SLOTS)
            dve.memset(top, NEVER).then_inc(setup, 1)
            dve.memset(hc, 0.0).then_inc(setup, 1)
            dve.memset(wtot, 0.0).then_inc(setup, 1)
            dve.wait_ge(made, 9)
            dve.tensor_copy(ident, identf).then_inc(setup, 1)
            dve.wait_ge(const_loaded, 64)
            dve.tensor_reduce(wmx, wcol, AX.X, ALU.max, apply_absolute_value=True).then_inc(setup, 1)
            norm_stats(0)
            s = Steps(dve, setup, 0, 11)
            s.n = 5
            dve.wait_ge(q_all, 1)
            s.link(dve.scalar_tensor_tensor(out=bound, in0=wmx[:, 1:2], scalar=32.0, in1=wmx[:, 0:1],
                                            op0=ALU.mult, op1=ALU.add))
            s.link(dve.tensor_scalar(bound, bound, TINY, None, ALU.max))
            scale_of(s, qscale, qp2, bound)
            s.step(dve.tensor_scalar(wq[:, 0, :], wcol[:, 0, :], qscale[:, 0:1], None, ALU.mult))
            s.link(dve.tensor_scalar(wq[:, 1, :], wcol[:, 1, :], qscale[:, 0:1], 1 / LN_SCALE, ALU.mult, ALU.mult))
            norm(0)
            norm_lo(0)
            for g in range(GROUPS):
                dve.wait_ge(ctx_loaded[g], 16)
                dve.tensor_reduce(cmax[:, g * GT:(g + 1) * GT], raw[:, g * GT:(g + 1) * GT, :], AX.X, ALU.max,
                                  apply_absolute_value=True)
                if g == 0:
                    for q in range(QT):
                        query(0, q)
                        query_lo(0, q)
            dve.wait_ge(tail_loaded, 16)
            dve.tensor_reduce(cmax[:, JT - 1:JT], raw[:, JT - 1, :], AX.X, ALU.max,
                              apply_absolute_value=True).then_inc(setup, 1)
            dve.wait_ge(setup, 12)
            s = Steps(dve, g_step, 0, 7)
            s.step(dve.tensor_reduce(gmax, cmax, AX.X, ALU.max))
            dve.wait_ge(g_all, 1)
            s.link(dve.tensor_scalar(gmax, gmax, TINY, None, ALU.max))
            scale_of(s, gscale, gp2, gmax)
            s.step(dve.tensor_copy(cscale_g, gscale))
            s.link(dve.tensor_scalar(cinv_g, gp2, 2.0 ** -TOP, None, ALU.mult))
            s.link(dve.tensor_scalar(sinv, qp2, cinv_g, 2.0 ** -TOP, ALU.mult, ALU.mult))
            split_pair(0)
            for t in range(NP):
                if t + 1 < NP:
                    split_pair(t + 1)
                if t >= 1:
                    running_max(0, t - 1)
                if t == 1:
                    norm_stats(1)
                if t == 3:
                    norm(1)
                if t == 4:
                    norm_lo(1)
            running_max(0, NP - 1)
            for q in range(QT):
                query(1, q)
                query_lo(1, q)
            iteration(1, first=True)
            with dve.Fori(2, NB - 1) as b:
                iteration(b)
            iteration(NB - 1, norms=False)
            iteration(NB, last=True, norms=False)
            take_acc(NB - 1)
            for k in range(KD):
                products(NB - 1, k)
                lows(NB - 1, k)

        @block.scalar
        def _(act):
            def split_pair(t):
                for h in range(2):
                    j = 2 * t + h
                    if t:
                        act.wait_ge(ct_done, j + 1)
                        act.wait_ge(c_kept, j - 1)
                    act.activation(ch[:, h, 0, :], raw[:, j, :], ACT.Identity, bias=zero[:, 0:1],
                                   scale=gscale[:, 0:1]).then_inc(c_hi, 1)

            def turned(t):
                act.wait_ge(ct_done, 2 * t + 3)
                act.copy(ctxT[:, :, :, 2 * t * P:(2 * t + 1) * P],
                         psT[0].rearrange("p (s k) i -> p s k i", s=2)).then_inc(ct_act, 1)

            def norm_sd(b):
                act.wait_ge(ln_step, LK * b + 2 * QT)
                act.activation(sd, mv[:, :, 1], ACT.Sqrt, bias=lneps[:, 0:1], scale=1 / LN_SCALE ** 2)\
                   .then_inc(ln_sd, 1)

            def norm_hi(b):
                for q in range(QT):
                    act.wait_ge(ln_step, LK * b + 2 * QT + 2 + q)
                    act.copy(eh[:, q, 0, :], xs[:, q, :]).then_inc(ln_hi, 1)

            def norm_turned(b, q, old):
                if old and q == 0:
                    act.wait_ge(et_out, 16 * (b - 1))
                    act.wait_ge(e_step, EK * (b - 1))
                et = eT[:, bass.ds(b % 2, 1)].rearrange("p o s k i -> p (o s k) i")
                act.wait_ge(ln_t, QT * b + q + 1)
                act.copy(et[:, :, q * P:(q + 1) * P], psE).then_inc(et_ready, 1)

            def query_hi(b, q, old):
                if old and q == 0:
                    act.wait_ge(qk_done, NP * b)
                act.wait_ge(q_step, QK * b + (KD + 2) * q + KD + 1)
                act.copy(qT[:, 0, :, q * P:(q + 1) * P], es).then_inc(q_hi, 1)

            def scores(b, t):
                n = b * NP + t
                act.wait_ge(qk_done, n + 1)
                act.wait_ge(slot_free, n + 1)
                slot = S[:, bass.ds(n % SLOTS, 1)].rearrange("p o h i -> p (o h) i")
                bank = psS[:, bass.ds(n % 2, 1)].rearrange("p o h i -> p (o h) i")
                if t < NP - 1:
                    act.activation(slot, bank, ACT.Identity, bias=zero[:, 0:1], scale=sinv[:, 0:1])\
                       .then_inc(scores_ready, 1)
                else:
                    act.activation(slot[:, 0, :], bank[:, 0, :], ACT.Identity, bias=zero[:, 0:1], scale=sinv[:, 0:1])
                    act.activation(slot[:, 1, :], bank[:, 1, :], ACT.Identity, bias=pad[:, 0:1], scale=sinv[:, 0:1])\
                       .then_inc(scores_ready, 1)

            def probabilities(a):
                slot = S[:, bass.ds(a % SLOTS, 1)].rearrange("p o h i -> p (o h) i")
                act.wait_ge(sub_done, a + 1)
                act.activation(slot, slot, ACT.Exp).then_inc(exp_done, 1)
                act.wait_ge(av_done, a + 1)
                act.wait_ge(exp_done, a + 1)
                act.activation(prob[:, bass.ds(a % 3, 1), 0].rearrange("p o h i -> p (o h) i"), slot,
                               ACT.Copy, scale=P_SCALE).then_inc(hi_done, 1)

            def high_hq(c, k):
                if k == 0:
                    act.wait_ge(acc_step, ACK * (c + 1))
                    act.wait_ge(f_out, 16 * (c + 1))
                act.copy(feat[:, 0, 0, k, :], hq[:, k, :]).then_inc(f_hi, 1)

            def high_eh(c, k):
                act.wait_ge(f_eh, KD * c + k + 1)
                act.copy(feat[:, 1, 0, k, :], ehs[:, k % 2, :]).then_inc(f_hi, 1)

            def iteration(b, first=False, last=False, norms=True):
                a0 = NP * (b - 1)
                if first:
                    scores(b, 0)
                act.wait_ge(mb_done, b)
                act.copy(Mb, psC.rearrange("p (n i) -> p n i", n=2)).then_inc(mb_ready, 1)
                if not first and not last:
                    scores(b, 0)
                probabilities(a0)
                if not last:
                    scores(b, 1)
                probabilities(a0 + 1)
                if not last:
                    for t in range(2, AHEAD):
                        scores(b, t)
                act.wait_ge(hc_step, HK * (b - 1) + 3)
                act.activation(rr, top, ACT.Exp, bias=neg[:, 0:1]).then_inc(hc_w, 1)
                act.activation(wrow, Mb[:, 1, :], ACT.Exp, bias=neg[:, 0:1], accum_out=ws).then_inc(hc_w, 1)
                for t in range(NP):
                    if t + 2 < NP:
                        probabilities(a0 + t + 2)
                    if not first and t < KD:
                        high_hq(b - 2, t)
                        high_eh(b - 2, t)
                    if norms:
                        if t == 1:
                            norm_sd(b + 1)
                        if t == 3:
                            norm_hi(b + 1)
                        if t in (6, 10):
                            norm_turned(b + 1, (t - 6) // 4, True)
                        if t in (9, 12):
                            query_hi(b + 1, (t - 9) // 3, True)
                    if not last and t + AHEAD < NP:
                        scores(b, t + AHEAD)

            act.sem_inc(scores_ready, 2)
            act.wait_ge(made, 9)
            norm_sd(0)
            norm_hi(0)
            for q in range(QT):
                norm_turned(0, q, False)
            for q in range(QT):
                query_hi(0, q, False)
            act.wait_ge(g_step, 7)
            split_pair(0)
            for t in range(NP):
                if t + 1 < NP:
                    split_pair(t + 1)
                turned(t)
                if t >= 1:
                    scores(0, t - 1)
                if t == 2:
                    norm_sd(1)
                if t == 4:
                    norm_hi(1)
                if t in (6, 7):
                    norm_turned(1, t - 6, False)
            scores(0, NP - 1)
            for q in range(QT):
                query_hi(1, q, True)
            iteration(1, first=True)
            with act.Fori(2, NB - 1) as b:
                iteration(b)
            iteration(NB - 1, norms=False)
            iteration(NB, last=True, norms=False)
            for k in range(KD):
                high_hq(NB - 1, k)
                high_eh(NB - 1, k)

        @block.tensor
        def _(pe):
            def turn_e(b, q):
                pe.wait_ge(ln_step, LK * b + 3 * QT + 2 + q)
                if q:
                    pe.wait_ge(et_ready, QT * b + q)
                for s in range(2):
                    for k in range(KD):
                        mm = pe.transpose(psE[:, s * KD + k, :], eh[:, q, s, k * P:(k + 1) * P], ident)
                mm.then_inc(ln_t, 1)

            def turn_ctx(t):
                for h in range(2):
                    pe.wait_ge(c_lo, 2 * t + h + 1)
                    if t:
                        pe.wait_ge((ct_act, ct_dve)[h], t)
                    for s in range(2):
                        for k in range(KD):
                            mm = pe.transpose(psT[h][:, s * KD + k, :], ch[:, h, s, k * P:(k + 1) * P], ident)
                    mm.then_inc(ct_done, 1)

            def scores(b, t):
                n = b * NP + t
                pe.wait_ge(scores_ready, n + 1)
                for h in range(2):
                    out = psS[:, bass.ds(n % 2, 1), h, :].rearrange("p o i -> p (o i)")
                    for k in range(KD):
                        for s, r in ((0, 0), (0, 1), (1, 0)):
                            mm = pe.matmul(out, ctxT[:, s, k, (2 * t + h) * P:(2 * t + h + 1) * P], qT[:, r, k, :],
                                           start=(k == 0 and s + r == 0), stop=(k == KD - 1 and s == 1))
                mm.then_inc(qk_done, 1)

            def products(b, t):
                a = (b - 1) * NP + t
                pe.wait_ge(p_ready, a + 1)
                for h in range(2):
                    for k in range(KD):
                        for s, r in ((0, 0), (0, 1), (1, 0)):
                            mm = pe.matmul(
                                psA[:, k, :], ctxN[:, 2 * t + h, s, k * P:(k + 1) * P],
                                prob[:, bass.ds(a % 3, 1), r, h, :].rearrange("p o i -> p (o i)"),
                                start=(t + h + s + r == 0), stop=(t == NP - 1 and h == 1 and s == 1))
                mm.then_inc(av_done, 1)

            def sums(c):
                pe.wait_ge(slot_free, SLOTS + NP * (c + 1))
                for h in range(2):
                    mm = pe.matmul(psL, onesf, L[:, h, :], start=(h == 0), stop=(h == 1))
                mm.then_inc(lsum_done, 1)

            def turn_maxima(c):
                pe.wait_ge(merge_done, c + 1)
                for q in range(QT):
                    mm = pe.transpose(psC[:, q * P:(q + 1) * P], Mc[:, q * P:(q + 1) * P], identf)
                mm.then_inc(mT_done, 1)

            def spread_maxima(c):
                pe.wait_ge(dg_step, DK * (c + 1))
                pe.matmul(psC, onesf, dg.rearrange("p n q i -> p (n q i)"), start=True, stop=True)\
                  .then_inc(mb_done, 1)

            def iteration(b, first=False, last=False, norms=True):
                if not last:
                    pe.wait_ge(q_step, QK * (b + 1))
                if first:
                    turn_maxima(0)
                else:
                    sums(b - 2)
                if not last:
                    scores(b, 0)
                    if first:
                        spread_maxima(0)
                    for t in range(1, AHEAD):
                        scores(b, t)
                if not first:
                    pe.wait_ge(acc_step, ACK * (b - 1))
                if first:
                    pe.wait_ge(c_kept, JT)
                for t in range(NP):
                    products(b, t)
                    if not last and t + AHEAD < NP:
                        scores(b, t + AHEAD)
                    if norms and t in (5, 7):
                        turn_e(b + 1, (t - 5) // 2)
                    if not last:
                        if t == 9:
                            turn_maxima(b)
                        if t == 12:
                            spread_maxima(b)

            pe.sem_inc(av_done, 3)
            pe.sem_inc(ct_done, 2)
            pe.wait_ge(setup, 4)
            for q in range(QT):
                turn_e(0, q)
            turn_ctx(0)
            for t in range(NP):
                if t + 1 < NP:
                    turn_ctx(t + 1)
                pe.wait_ge(ct_act, t + 1)
                pe.wait_ge(ct_dve, t + 1)
                if t == 0:
                    pe.wait_ge(q_step, QK)
                scores(0, t)
                if t in (5, 6):
                    turn_e(1, t - 5)
            iteration(1, first=True)
            with pe.Fori(2, NB - 1) as b:
                iteration(b)
            iteration(NB - 1, norms=False)
            iteration(NB, last=True, norms=False)
            sums(NB - 1)


def merge_and_route(nc, ps, arena, cst, x, w_qv, b_qv, g_x, g_f, w_r, b_r, feats, rows, x1_out, hc_in, ew):
    D = x.shape[1]
    KD = D // P
    NI = x.shape[0]
    IB = 256
    NB, QT = NI // IB, IB // P
    E = w_r.shape[1]
    CAP = rows.shape[0] // E
    NS = E * CAP
    FT = 3 * KD
    ROW = rows.shape[1]
    LAST = 3
    assert ew.CH == 4 * LAST - 4
    FAR = 8192.0
    take, _ = cutter(arena[:, :EARLY])

    Wt = take([FT, 2, D], F16)
    ft = [take([3, 2, KD, IB], F16) for _ in range(2)]
    W = take([4 * KD, D], F32)
    x2 = [take([QT, D], F32) for _ in range(2)]
    xn = take([QT, D], F32)
    row = [take([QT, ROW], F32) for _ in range(2)]
    halves = [r.bitcast(F16) for r in row]
    xT = take([QT, 2, KD, P], F16)
    bqb, brb = take([D], F32), take([E], F32)
    wr, wrs = take([KD, E], F32), take([KD, 2, E], F16)
    mx = take([5], F32)
    u, up2, sig, rp2, rsc = (take([1], F32) for _ in range(5))
    sc3 = take([3], F32)
    cY, cR, tx, tf, rw = (take([1], F32) for _ in range(5))
    gx, gf = take([1], F32), take([1], F32)
    hcn = take([KD], F32)
    t1 = take([2], F32)
    stats, mv, sd, rs = take([QT, 6], F32), take([QT, 2], F32), take([QT], F32), take([QT], F32)
    lneps = take([1], F32)
    iota8, tok = take([E], F32), take([NI // P], U32)
    lg, ex, gt = take([QT, E], F32), take([QT, E], F32), take([QT, E], F32)
    lm, lsum, lr = take([QT], F32), take([QT], F32), take([QT], F32)
    m8, ix = take([QT, 8], F32), take([QT, 8], U32)
    ixf = take([2, QT], F32)
    oh = take([2, QT, E], F32)
    mask = take([QT, E], F16)
    count = take([E], F32)
    base, pos, ohp = take([QT, E], F32), take([QT, E], F32), take([2, QT, E], F32)
    pk, kp, dst, away = (take([2, QT], F32) for _ in range(4))
    dsti = [take([2, QT], U32) for _ in range(2)]
    wk, wsum, wi = take([2, QT], F32), take([QT], F32), take([QT], F32)
    tri, ones = take([P], F16), take([P], F16)
    trif = take([P], F32)
    ident = cst["ident"]
    hc, wtot, cinv, cscale = hc_in["hc"], hc_in["wtot"], hc_in["ctx_inv"], hc_in["ctx_scale"]

    psY = [ps[:, 0:2, :], ps[:, 6:8, :]]
    psR = [ps[:, n, :].bitcast(F16).rearrange("p (c i) -> p c i", i=P) for n in (2, 5)]
    psG = ps[:, 3, 0:QT * E].rearrange("p (i e) -> p i e", e=E)
    psK = ps[:, 4, 0:2 * QT * E].rearrange("p (n e) -> p n e", e=E)
    psB = ps[:, 4, 0:P]

    with ExitStack() as st:
        def sem(name):
            return st.enter_context(nc.semaphore(name))

        w_loaded, p_loaded, made, mx_done, mx_all, prep, w_hi, w_lo, t_done = (sem(s) for s in (
            "w_loaded", "p_loaded", "made2", "mx_done", "mx_all", "prep", "w_hi", "w_lo", "t_done"))
        f_loaded = [sem("f_loaded_0"), sem("f_loaded_1")]
        x_loaded = [sem("x2_loaded_0"), sem("x2_loaded_1")]
        x_stored = [sem("x1_stored_0"), sem("x1_stored_1")]
        y_done, y_step, sd_done, hi_done, turned, xt_ready, logits, e_done, r_step, counted = (sem(s) for s in (
            "y_done", "y_step", "sd_done", "row_hi", "turned", "xt_ready", "logits", "e_done", "r_step",
            "counted"))
        sent, row_free = [[sem(f"{name}_{v}") for v in range(2)] for name in ("sent", "row_free")]
        sp_passed, dve_passed, pool_passed = (sem(f"{e}_passed_2") for e in ("sp", "dve", "pool"))
        block = st.enter_context(nc.Block())
        YK = 2 * QT + 2 * QT + 1 + 2 * QT
        R1 = 9 + 2 * QT
        RK = R1 + 17 + QT

        @block.sync
        def _(sp):
            sp.dma_start(W, w_qv.rearrange("(c p) d -> p c d", p=P)).then_inc(w_loaded, 16)
            sp.dma_start(bqb, b_qv.partition_broadcast(P)).then_inc(p_loaded, 16)
            sp.dma_start(brb, b_r.partition_broadcast(P)).then_inc(p_loaded, 16)
            sp.dma_start(gx, g_x.partition_broadcast(P)).then_inc(p_loaded, 16)
            sp.dma_start(gf, g_f.partition_broadcast(P)).then_inc(p_loaded, 16)
            sp.dma_start(wr, w_r.rearrange("(k p) e -> p k e", p=P)).then_inc(p_loaded, 16)
            sp.dma_start(ew.b1n, ew.b1.rearrange("e (f p) -> (e f) p", p=P)).then_inc(ew.b1_loaded, 16)

            def load(b, v):
                sp.dma_start(ft[v].rearrange("p f s k i -> p (f s k i)"),
                             feats[bass.ds(b, 1)].rearrange("o p f c -> (o p) (f c)")).then_inc(f_loaded[v], 16)
                sp.dma_start(x2[v], x[bass.ds(b * IB, IB), :].rearrange("(q p) d -> p q d", p=P))\
                    .then_inc(x_loaded[v], 16)

            def store(b, v, n):
                sp.wait_ge(y_step, YK * b + 2 * QT)
                apart(sp, sp_passed)
                sp.dma_start(x1_out[bass.ds(b * IB, IB), :].rearrange("(q p) d -> p q d", p=P), x2[v])\
                    .then_inc(x_stored[v], 16)
                sp.wait_ge(x_stored[v], 16 * (n + 1))
                apart(sp, sp_passed)

            load(0, 0)
            load(1, 1)
            ew.load(sp, 0, False)
            with sp.Fori(0, NB // 2 - 1) as n:
                for v in range(2):
                    store(2 * n + v, v, n)
                    sp.wait_ge(y_step, YK * (2 * n + v + 1))
                    apart(sp, sp_passed)
                    sp.wait_ge(y_done, QT * (2 * n + v + 1))
                    load(2 * n + v + 2, v)
            for v in range(2):
                store(NB - 2 + v, v, NB // 2 - 1)

        @block.gpsimd
        def _(pool):
            pool.memset(lneps, LN_EPS / LN_SCALE ** 2).then_inc(made, 1)
            pool.memset(trif, 1.0).then_inc(made, 1)
            pool.iota(tok, pattern=[[P, NI // P]], base=0, channel_multiplier=1).then_inc(made, 1)
            pool.iota(iota8, pattern=[[1, E]], base=0, channel_multiplier=0,
                      allow_small_or_imprecise_dtypes=True).then_inc(made, 1)
            pool.wait_ge(made, 4)
            pool.affine_select(out=trif, in_=trif, compare_op=ALU.is_gt, fill=0.0, base=0,
                               pattern=[[1, P]], channel_multiplier=-1).then_inc(made, 1)
            pool.sem_inc(row_free[0], 1)
            pool.sem_inc(row_free[1], 1)
            pool.wait_ge(mx_done, 5)
            pool.partition_all_reduce(mx, mx, P, RMAX).then_inc(mx_all, 1)
            pool.iota(ew.en, pattern=[[1, E]], base=0, channel_multiplier=0,
                      allow_small_or_imprecise_dtypes=True).then_inc(ew.en_made, 1)
            pool.wait_ge(ew.init, 1)
            pool.partition_all_reduce(ew.mb, ew.mb, P, RMAX).then_inc(ew.en_made, 1)

            def send(n):
                for v in range(2):
                    pool.wait_ge(r_step, RK * (2 * n + v + 1))
                    apart(pool, pool_passed)
                    for q in range(QT):
                        for k in range(2):
                            pool.indirect_dma_start(
                                out=rows, out_offset=bass.IndirectOffsetOnAxis(ap=dsti[v][:, k, q:q + 1], axis=0),
                                in_=row[v][:, q, :], in_offset=None, bounds_check=NS - 1, oob_is_err=False)\
                                .then_inc(sent[v], 16)
                    pool.wait_ge(sent[v], 32 * QT * (n + 1))
                    pool.sem_inc(row_free[v], 1)

            with pool.Fori(0, NB // 2 - LAST) as n:
                send(n)
            ew.reduce_max(pool, 0)
            with pool.Fori(NB // 2 - LAST, NB // 2) as n:
                send(n)

        @block.vector
        def _(dve):
            def y_part(b, v, q):
                s = Steps(dve, y_step, b, YK)
                s.n = 2 * q
                dve.wait_ge(y_done, QT * b + q + 1)
                s.link(dve.tensor_tensor(x2[v][:, q, :], x2[v][:, q, :], bqb, ALU.add))
                s.step(dve.scalar_tensor_tensor(out=x2[v][:, q, :], in0=psY[v][:, q, :], scalar=cY[:, 0:1],
                                                in1=x2[v][:, q, :], op0=ALU.mult, op1=ALU.add))

            def norm_part(b, v, n):
                s = Steps(dve, y_step, b, YK)
                s.n = 2 * QT
                s.wait()
                for q in range(QT):
                    s.step(dve.bn_stats(stats[:, q, :], x2[v][:, q, :]))
                s.wait()
                apart(dve, dve_passed)
                for q in range(QT):
                    s.step(dve.bn_aggr(mv[:, q, :], stats[:, q, :]))
                dve.wait_ge(sd_done, b + 1)
                s.link(dve.reciprocal(rs, sd))
                for q in range(QT):
                    s.step(dve.tensor_scalar(xn[:, q, :], x2[v][:, q, :], mv[:, q, 0:1], rs[:, q:q + 1],
                                             ALU.subtract, ALU.mult))
                for q in range(QT):
                    dve.wait_ge(hi_done, QT * b + q + 1)
                    s.step(dve.tensor_tensor(halves[v][:, q, D:2 * D], xn[:, q, :], halves[v][:, q, 0:D], ALU.subtract))
                assert s.n == YK

            def route_1(c):
                s = Steps(dve, r_step, c, RK)
                dve.wait_ge(logits, c + 1)
                s.link(dve.scalar_tensor_tensor(out=lg, in0=psG, scalar=cR[:, 0:1], in1=bcast(brb, QT),
                                                op0=ALU.mult, op1=ALU.add))
                s.link(dve.tensor_reduce(lm, lg, AX.X, ALU.max))
                s.link(dve.tensor_tensor(lg, lg, spread(lm, E), ALU.subtract))
                dve.wait_ge(e_done, c + 1)
                s.link(dve.tensor_reduce(lsum, ex, AX.X, ALU.add))
                s.link(dve.reciprocal(lr, lsum))
                s.link(dve.tensor_tensor(gt, ex, spread(lr, E), ALU.mult))
                apart(dve, dve_passed)
                for q in range(QT):
                    s.step(dve.max(m8[:, q, :], gt[:, q, :]))
                s.wait()
                apart(dve, dve_passed)
                for q in range(QT):
                    s.step(dve.max_index(ix[:, q, :], m8[:, q, :], gt[:, q, :]))
                s.wait()
                s.link(dve.tensor_copy(ixf, ix[:, :, 0:2].rearrange("p q k -> p k q")))
                s.link(dve.tensor_tensor(oh.rearrange("p k q e -> p (k q) e"), bcast(iota8, 2 * QT),
                                         spread(ixf.rearrange("p k q -> p (k q)"), E), ALU.is_equal))
                s.step(dve.tensor_tensor(mask, oh[:, 0], oh[:, 1], ALU.add))
                assert s.n == R1

            def route_2(c, v, n):
                s = Steps(dve, r_step, c, RK)
                s.n = R1
                dve.wait_ge(counted, c + 1)
                s.link(dve.tensor_copy(base[:, 0, :], count))
                for q in range(1, QT):
                    s.link(dve.tensor_tensor(base[:, q, :], base[:, q - 1, :], psK[:, QT + q - 1, :], ALU.add))
                s.step(dve.tensor_tensor(count, base[:, QT - 1, :], psK[:, 2 * QT - 1, :], ALU.add))
                s.link(dve.tensor_tensor(pos, psK[:, 0:QT, :], base, ALU.add))
                for k in range(2):
                    s.step(dve.tensor_tensor(ohp[:, k], oh[:, k], pos, ALU.mult))
                s.wait()
                s.link(dve.tensor_reduce(pk, ohp, AX.X, ALU.add))
                s.step(dve.tensor_scalar(kp, pk, float(CAP), None, ALU.is_lt))
                s.link(dve.tensor_scalar(away, pk, float(CAP), FAR, ALU.is_ge, ALU.mult))
                s.link(dve.scalar_tensor_tensor(out=dst, in0=ixf, scalar=float(CAP), in1=pk,
                                                op0=ALU.mult, op1=ALU.add))
                dve.wait_ge(row_free[v], n + 1)
                s.step(dve.tensor_tensor(dsti[v], dst, away, ALU.add))
                s.link(dve.tensor_tensor(wk, kp, m8[:, :, 0:2].rearrange("p q k -> p k q"), ALU.mult))
                s.link(dve.tensor_tensor(wsum, wk[:, 0, :], wk[:, 1, :], ALU.add))
                s.link(dve.tensor_scalar(wsum, wsum, 1e-6, None, ALU.max))
                s.link(dve.reciprocal(wi, wsum))
                s.link(dve.tensor_scalar(wi, wi, tf[:, 0:1], None, ALU.mult))
                info = row[v][:, :, D:D + 4]
                s.step(dve.tensor_copy(info[:, :, 0:1].bitcast(U32).rearrange("p q o -> p (q o)"),
                                       tok[:, bass.ds(c * QT, QT)]))
                s.step(dve.tensor_tensor(info[:, :, 1:3], wk.rearrange("p k q -> p q k"), spread(wi, 2), ALU.mult))
                s.step(dve.tensor_copy(info[:, :, 3], ixf[:, 0, :]))
                assert s.n == RK, (s.n, RK)

            dve.wait_ge(w_loaded, 16)
            dve.wait_ge(p_loaded, 80)
            for n in range(4):
                dve.tensor_reduce(mx[:, n:n + 1], W[:, n * KD:(n + 1) * KD, :].rearrange("p c d -> p (c d)"),
                                  AX.X, ALU.max, apply_absolute_value=True).then_inc(mx_done, 1)
            dve.tensor_reduce(mx[:, 4:5], wr.rearrange("p k e -> p (k e)"), AX.X, ALU.max,
                              apply_absolute_value=True).then_inc(mx_done, 1)
            dve.wait_ge(mx_all, 1)
            s = Steps(dve, prep, 0, 40)
            s.link(dve.scalar_tensor_tensor(out=t1[:, 0:1], in0=mx[:, 3:4], scalar=32.0, in1=mx[:, 0:1],
                                            op0=ALU.mult, op1=ALU.add))
            s.link(dve.tensor_scalar(t1[:, 0:1], t1[:, 0:1], 1 / LN_SCALE, TINY, ALU.mult, ALU.max))
            s.link(dve.scalar_tensor_tensor(out=t1[:, 1:2], in0=mx[:, 2:3], scalar=32.0, in1=mx[:, 1:2],
                                            op0=ALU.mult, op1=ALU.max))
            s.link(dve.scalar_tensor_tensor(out=u, in0=t1[:, 1:2], scalar=cinv, in1=t1[:, 0:1],
                                            op0=ALU.mult, op1=ALU.max))
            s.link(dve.tensor_scalar(up2.bitcast(I32), u.bitcast(I32), EXPONENT, None, ALU.bitwise_and))
            s.link(dve.tensor_scalar(sig.bitcast(I32), up2.bitcast(I32), -1, float((254 + TOP) << 23),
                                     ALU.mult, ALU.add))
            s.step(dve.tensor_scalar(sc3[:, 0:1], sig, 1 / LN_SCALE, None, ALU.mult))
            s.step(dve.tensor_scalar(sc3[:, 1:2], sig, cinv, None, ALU.mult))
            s.step(dve.tensor_scalar(sc3[:, 2:3], sig, cinv, 32.0, ALU.mult, ALU.mult))
            s.link(dve.tensor_scalar(t1[:, 0:1], mx[:, 4:5], TINY, None, ALU.max))
            s.link(dve.tensor_scalar(rp2.bitcast(I32), t1[:, 0:1].bitcast(I32), EXPONENT, None, ALU.bitwise_and))
            s.step(dve.tensor_scalar(cR, rp2, 2.0 ** -TOP / LN_SCALE, None, ALU.mult))
            s.link(dve.tensor_scalar(rsc.bitcast(I32), rp2.bitcast(I32), -1, float((254 + TOP) << 23),
                                     ALU.mult, ALU.add))
            s.link(dve.tensor_scalar(wrs[:, :, 0, :], wr, rsc[:, 0:1], None, ALU.mult))
            s.step(dve.scalar_tensor_tensor(out=wrs[:, :, 1, :], in0=wr, scalar=rsc[:, 0:1], in1=wrs[:, :, 0, :],
                                            op0=ALU.mult, op1=ALU.subtract))
            s.link(dve.reciprocal(rw, wtot))
            s.link(dve.tensor_scalar(hcn, hc, rw[:, 0:1], 1 / LN_SCALE, ALU.mult, ALU.mult))
            for k in range(KD):
                s.step(dve.scalar_tensor_tensor(out=W[:, k, :], in0=W[:, 3 * KD + k, :], scalar=hcn[:, k:k + 1],
                                                in1=W[:, k, :], op0=ALU.mult, op1=ALU.add))
            dve.wait_ge(t_done, 2)
            s.step(dve.tensor_scalar(cY, up2, tx[:, 0:1], 2.0 ** -TOP, ALU.mult, ALU.mult))
            s.step(dve.tensor_scalar(bqb, bqb, tx[:, 0:1], None, ALU.mult))
            dve.wait_ge(made, 5)
            s.step(dve.tensor_copy(tri, trif))
            s.step(dve.memset(ones, 1.0))
            s.step(dve.memset(count, 0.0))
            for v in range(2):
                s.step(dve.memset(row[v][:, :, D:D + 4], 0.0))
            ready = s.n
            s.wait()
            for k in range(FT):
                dve.wait_ge(w_hi, k + 1)
                dve.scalar_tensor_tensor(out=Wt[:, k, 1, :], in0=W[:, k, :], scalar=sc3[:, k // KD:k // KD + 1],
                                         in1=Wt[:, k, 0, :], op0=ALU.mult, op1=ALU.subtract).then_inc(w_lo, 1)

            def body(b, v, n, routed=True):
                dve.wait_ge(x_loaded[v], 16 * (n + 1))
                y_part(b, v, 0)
                if routed:
                    route_1(b - 1)
                y_part(b, v, 1)
                norm_part(b, v, n)
                if routed:
                    route_2(b - 1, 1 - v, n if v else n - 1)

            dve.wait_ge(ew.b1_loaded, 16)
            dve.tensor_reduce(ew.mb, ew.b1n, AX.X, ALU.max, apply_absolute_value=True).then_inc(ew.init, 1)
            dve.wait_ge(ew.b1_turned, 1)
            dve.tensor_copy(ew.b1T, psB).then_inc(ew.init, 1)
            body(0, 0, 0, routed=False)
            body(1, 1, 0)
            with dve.Fori(1, NB // 2 - LAST) as n:
                body(2 * n, 0, n)
                body(2 * n + 1, 1, n)
            dve.wait_ge(ew.en_made, 2)
            for n in range(NB // 2 - LAST, NB // 2):
                for v in range(2):
                    body(2 * n + v, v, n)
                    m = 2 * (n - NB // 2 + LAST) + v
                    for c in (2 * m, 2 * m + 1):
                        if m < 2:
                            ew.max_part(dve, 0, c)
                        else:
                            ew.low_part(dve, 0, c - 4, False)
                    if m == 1:
                        ew.scales(dve, 0, False)
            route_1(NB - 1)
            route_2(NB - 1, 1, NB // 2 - 1)

        @block.scalar
        def _(act):
            act.wait_ge(p_loaded, 80)
            act.activation(tx, gx, ACT.Tanh).then_inc(t_done, 1)
            act.activation(tf, gf, ACT.Tanh).then_inc(t_done, 1)
            for k in range(FT):
                if k == 0:
                    act.wait_ge(prep, 17 + KD)
                act.mul(Wt[:, k, 0, :], W[:, k, :], sc3[:, k // KD:k // KD + 1]).then_inc(w_hi, 1)

            def body(b, v, n, routed=True):
                if routed:
                    c = b - 1
                    for q in range(QT):
                        act.wait_ge(turned, QT * c + q + 1)
                        act.copy(xT[:, q].rearrange("p s k i -> p (s k) i"), psR[q]).then_inc(xt_ready, 1)
                    act.wait_ge(r_step, RK * c + 3)
                    act.activation(ex, lg, ACT.Exp).then_inc(e_done, 1)
                act.wait_ge(y_step, YK * b + 4 * QT)
                act.activation(sd, mv[:, :, 1], ACT.Sqrt, bias=lneps[:, 0:1], scale=1 / LN_SCALE ** 2)\
                   .then_inc(sd_done, 1)
                act.wait_ge(row_free[v], n + 1)
                for q in range(QT):
                    act.wait_ge(y_step, YK * b + 4 * QT + 2 + q)
                    act.copy(halves[v][:, q, 0:D], xn[:, q, :]).then_inc(hi_done, 1)

            def tail(c):
                for q in range(QT):
                    act.wait_ge(turned, QT * c + q + 1)
                    act.copy(xT[:, q].rearrange("p s k i -> p (s k) i"), psR[q]).then_inc(xt_ready, 1)
                act.wait_ge(r_step, RK * c + 3)
                act.activation(ex, lg, ACT.Exp).then_inc(e_done, 1)

            act.wait_ge(made, 5)
            body(0, 0, 0, routed=False)
            body(1, 1, 0)
            with act.Fori(1, NB // 2 - LAST) as n:
                body(2 * n, 0, n)
                body(2 * n + 1, 1, n)
            for n in range(NB // 2 - LAST, NB // 2):
                for v in range(2):
                    body(2 * n + v, v, n)
                    m = 2 * (n - NB // 2 + LAST) + v
                    if m >= 2:
                        for c in (2 * m - 4, 2 * m - 3):
                            ew.high_part(act, 0, c, False)
            tail(NB - 1)

        @block.tensor
        def _(pe):
            def merge(b, v, q, part, first=False, old=True):
                if old and part == 0:
                    pe.wait_ge(y_step, YK * (b - 2) + 2 * q + 2)
                for k in range(part * FT // 2, (part + 1) * FT // 2):
                    if first:
                        pe.wait_ge(w_lo, k + 1)
                    for s, r in ((0, 0), (0, 1), (1, 0)):
                        mm = pe.matmul(psY[v][:, q, :], ft[v][:, k // KD, s, k % KD, q * P:(q + 1) * P], Wt[:, k, r, :],
                                       start=(k + s + r == 0), stop=(k == FT - 1 and s == 1))
                if part == 1:
                    mm.then_inc(y_done, 1)

            def turn_rows(c, v):
                for q in range(QT):
                    pe.wait_ge(y_step, YK * c + 5 * QT + 2 + q)
                    for s in range(2):
                        for k in range(KD):
                            mm = pe.transpose(psR[q][:, s * KD + k, :],
                                              halves[v][:, q, s * D + k * P:s * D + (k + 1) * P], ident)
                    mm.then_inc(turned, 1)

            def router(c):
                pe.wait_ge(xt_ready, QT * (c + 1))
                for q in range(QT):
                    for k in range(KD):
                        for s, r in ((0, 0), (0, 1), (1, 0)):
                            mm = pe.matmul(psG[:, q, :], xT[:, q, s, k, :], wrs[:, k, r, :],
                                           start=(k + s + r == 0), stop=(k == KD - 1 and s == 1))
                mm.then_inc(logits, 1)

            def counts(c):
                pe.wait_ge(r_step, RK * c + R1)
                pe.matmul(psK[:, 0:QT, :], tri, mask, start=True, stop=True)
                pe.matmul(psK[:, QT:2 * QT, :], ones, mask, start=True, stop=True).then_inc(counted, 1)

            def body(b, v, n, routed=True, old=True):
                pe.wait_ge(f_loaded[v], 16 * (n + 1))
                merge(b, v, 0, 0, not routed, old)
                merge(b, v, 0, 1, not routed, old)
                if routed:
                    turn_rows(b - 1, 1 - v)
                merge(b, v, 1, 0, not routed, old)
                if routed:
                    router(b - 1)
                merge(b, v, 1, 1, not routed, old)
                if routed:
                    counts(b - 1)

            pe.wait_ge(ew.b1_loaded, 16)
            pe.transpose(psB, ew.b1n, cst["identf"]).then_inc(ew.b1_turned, 1)
            pe.wait_ge(prep, 24 + KD)
            body(0, 0, 0, routed=False, old=False)
            body(1, 1, 0, old=False)
            with pe.Fori(1, NB // 2) as n:
                body(2 * n, 0, n)
                body(2 * n + 1, 1, n)
            turn_rows(NB - 1, 1)
            router(NB - 1)
            counts(NB - 1)


def experts(nc, ps, arena, cst, ew, b2, rows, out):
    E, D, F, KD, KF, CH, SK = ew.E, ew.D, ew.F, ew.KD, ew.KF, ew.CH, ew.SK
    CAP = rows.shape[0] // E
    ST = CAP // P
    HALF = CAP // 2
    ROW = rows.shape[1]
    NT = out.shape[0]
    take, _ = cutter(arena[:, :EARLY])

    hT = take([KF, 2, CAP], F16)
    XT = take([2, KD, CAP], F16)
    Xr = take([ST, ROW], F32)
    Xh = Xr.bitcast(F16)
    h32 = [take([CAP], F32) for _ in range(2)]
    w2s = ew.w2s = take([2, KF * D], F16)
    w1s = ew.w1s
    b2b = take([D], F32)
    o32 = [take([D], F32) for _ in range(2)]
    oa = [take([D], F32) for _ in range(2)]
    eq, da = take([ST], F32), take([ST], F32)
    al, tk = [take([ST], F32) for _ in range(2)], [take([ST], U32) for _ in range(2)]
    ident = cst["ident"]
    b1T, en, inv1, inv2, sh, s_step, s_lo = ew.b1T, ew.en, ew.inv1, ew.inv2, ew.sh, ew.s_step, ew.s_lo

    psH = ps[:, 0:4, 0:HALF].rearrange("p (v h) i -> p v h i", h=2)
    psO = ps[:, 4:6, :]
    psX = [ps[:, n, :].bitcast(F16).rearrange("p (c i) -> p c i", i=P) for n in (6, 7)]

    with ExitStack() as st:
        def sem(name):
            return st.enter_context(nc.semaphore(name))

        x_loaded, x_turned, xt_ready, a_step = (sem(s) for s in ("rows_loaded", "x_turned", "xt3_ready", "a_step"))
        h_done, g_done, h_hi, h_lo = (sem(s) for s in ("h_done", "g_done", "h_hi", "h_lo"))
        o_done, o_bias, o_scaled, added, b2_loaded = (sem(s) for s in (
            "o_done", "o_bias", "o_scaled", "added", "b2_loaded"))
        sp_passed = sem("sp_passed_3")
        block = st.enter_context(nc.Block())
        AK = 7

        @block.sync
        def _(sp):
            def load_rows(e):
                sp.dma_start(Xr, rows[bass.ds(e * CAP, CAP), :].rearrange("(t p) c -> p t c", p=P))\
                    .then_inc(x_loaded, 16)

            def load_b2(e):
                sp.dma_start(b2b, b2[bass.ds(e, 1), :].partition_broadcast(P).rearrange("p o d -> p (o d)"))\
                    .then_inc(b2_loaded, 16)

            load_rows(0)
            load_b2(0)
            sp.wait_ge(s_lo, CH)
            ew.load(sp, 0, True)
            with sp.Fori(0, E - 1) as e:
                sp.wait_ge(a_step, AK * (e + 1))
                apart(sp, sp_passed)
                sp.wait_ge(x_turned, ST * (e + 1))
                load_rows(e + 1)
                sp.wait_ge(s_lo, CH * (2 * e + 2))
                ew.load(sp, e + 1, False)
                sp.wait_ge(s_lo, CH * (2 * e + 3))
                ew.load(sp, e + 1, True)
                sp.wait_ge(o_bias, ST * (e + 1))
                load_b2(e + 1)

        @block.gpsimd
        def _(pool):
            def add_rows(e, more=True):
                for t in range(ST):
                    pool.wait_ge(o_scaled, ST * e + t + 1)
                    apart(pool, ew.pool_passed)
                    pool.indirect_dma_start(
                        out=out, out_offset=bass.IndirectOffsetOnAxis(ap=tk[1][:, t:t + 1], axis=0),
                        in_=oa[t % 2], in_offset=None, bounds_check=NT - 1, oob_is_err=False,
                        compute_op=ALU.add).then_inc(added, 16)
                    pool.wait_ge(added, 16 * (ST * e + t + 1))
                    if t == 1 and more:
                        ew.reduce_max(pool, 2 * e + 2)

            with pool.Fori(0, E - 1) as e:
                ew.reduce_max(pool, 2 * e + 1)
                add_rows(e)
            ew.reduce_max(pool, 2 * E - 1)
            add_rows(E - 1, more=False)

        @block.vector
        def _(dve):
            def weights_of(e):
                s = Steps(dve, a_step, e, AK)
                info = Xr[:, :, D:D + 4]
                dve.wait_ge(x_loaded, 16 * e + 16)
                s.step(dve.tensor_copy(tk[0], info[:, :, 0:1].bitcast(U32).rearrange("p t o -> p (t o)")))
                s.step(dve.tensor_scalar(eq, info[:, :, 3], en[:, bass.ds(e, 1)], None, ALU.is_equal))
                s.link(dve.tensor_tensor(da, info[:, :, 1], info[:, :, 2], ALU.subtract))
                s.link(dve.tensor_tensor(da, da, eq, ALU.mult))
                s.link(dve.tensor_tensor(al[0], da, info[:, :, 2], ALU.add))

            def keep_weights(e):
                s = Steps(dve, a_step, e, AK)
                s.n = 5
                s.step(dve.tensor_copy(al[1], al[0]))
                s.step(dve.tensor_copy(tk[1], tk[0]))

            def layer_1(e):
                for f in range(KF):
                    n = e * KF + f
                    if f < 4:
                        ew.max_part(dve, 2 * e + 1, f)
                    if f == 5:
                        ew.scales(dve, 2 * e + 1, True)
                    if 6 <= f < 6 + CH:
                        ew.low_part(dve, 2 * e + 1, f - 6, True)
                    dve.wait_ge(h_hi, n + 1)
                    dve.scalar_tensor_tensor(out=hT[:, f, 1, :], in0=h32[f % 2], scalar=sh[:, 0:1],
                                             in1=hT[:, f, 0, :], op0=ALU.mult, op1=ALU.subtract).then_inc(h_lo, 1)

            def layer_2(e, more=True):
                for t in range(ST):
                    n = e * ST + t
                    if t == 0:
                        dve.wait_ge(b2_loaded, 16 * (e + 1))
                    if t >= 2:
                        dve.wait_ge(o_scaled, n - 1)
                    dve.wait_ge(o_done, n + 1)
                    dve.scalar_tensor_tensor(out=o32[t % 2], in0=psO[:, t % 2, :], scalar=inv2[:, 0:1], in1=b2b,
                                             op0=ALU.mult, op1=ALU.add).then_inc(o_bias, 1)
                    if more:
                        if t < 2:
                            ew.max_part(dve, 2 * e + 2, 2 * t)
                            ew.max_part(dve, 2 * e + 2, 2 * t + 1)
                        if t == 2:
                            ew.scales(dve, 2 * e + 2, False)
                        if t in (2, 3):
                            for c in range(4):
                                ew.low_part(dve, 2 * e + 2, 4 * (t - 2) + c, False)

            weights_of(0)
            keep_weights(0)
            with dve.Fori(0, E - 1) as e:
                layer_1(e)
                layer_2(e)
                weights_of(e + 1)
                dve.wait_ge(added, 16 * ST * (e + 1))
                keep_weights(e + 1)
            layer_1(E - 1)
            layer_2(E - 1, more=False)

        @block.scalar
        def _(act):
            def turned(e, t):
                act.wait_ge(x_turned, ST * e + t + 1)
                act.copy(XT[:, :, :, t * P:(t + 1) * P], psX[t % 2].rearrange("p (s k) i -> p s k i", s=2))\
                   .then_inc(xt_ready, 1)

            def layer_1(e):
                for f in range(KF):
                    n = e * KF + f
                    act.wait_ge(h_done, n + 1)
                    if f == 0:
                        act.wait_ge(s_step, SK * (2 * e + 1))
                    if f >= 2:
                        act.wait_ge(h_lo, n - 1)
                    act.activation(h32[f % 2].rearrange("p (h i) -> p h i", h=2), psH[:, f % 2], ACT.Gelu,
                                   bias=b1T[:, bass.ds(n, 1)], scale=inv1[:, 0:1]).then_inc(g_done, 1)
                    act.wait_ge(g_done, n + 1)
                    act.mul(hT[:, f, 0, :], h32[f % 2], sh[:, 0:1]).then_inc(h_hi, 1)
                    if 5 <= f < 5 + CH:
                        ew.high_part(act, 2 * e + 1, f - 5, True)

            def layer_2(e, more=True):
                for t in range(ST):
                    n = e * ST + t
                    if more:
                        turned(e + 1, t)
                        if t in (2, 3):
                            for c in range(4):
                                ew.high_part(act, 2 * e + 2, 4 * (t - 2) + c, False)
                    act.wait_ge(o_bias, n + 1)
                    if t >= 2:
                        act.wait_ge(added, 16 * (n - 1))
                    act.mul(oa[t % 2], o32[t % 2], al[1][:, t:t + 1]).then_inc(o_scaled, 1)

            for t in range(ST):
                turned(0, t)
            with act.Fori(0, E - 1) as e:
                layer_1(e)
                layer_2(e)
            layer_1(E - 1)
            layer_2(E - 1, more=False)

        @block.tensor
        def _(pe):
            def turn(e, t):
                if t >= 2:
                    pe.wait_ge(xt_ready, ST * e + t - 1)
                elif t == 0:
                    pe.wait_ge(x_loaded, 16 * (e + 1))
                for s in range(2):
                    for k in range(KD):
                        mm = pe.transpose(psX[t % 2][:, s * KD + k, :], Xh[:, t, s * D + k * P:s * D + (k + 1) * P], ident)
                mm.then_inc(x_turned, 1)

            def layer_1(e):
                pe.wait_ge(xt_ready, ST * (e + 1))
                pe.wait_ge(s_lo, CH * (2 * e + 1))
                for f in range(KF):
                    n = e * KF + f
                    if f >= 2:
                        pe.wait_ge(g_done, n - 1)
                    for k in range(KD):
                        for s, r in ((0, 0), (0, 1), (1, 0)):
                            for h in range(2):
                                mm = pe.matmul(psH[:, f % 2, h, :], w1s[:, s, k * F + f * P:k * F + (f + 1) * P],
                                               XT[:, r, k, h * HALF:(h + 1) * HALF],
                                               start=(k + s + r == 0), stop=(k == KD - 1 and s == 1))
                    mm.then_inc(h_done, 1)

            def layer_2(e, more=True):
                pe.wait_ge(s_lo, CH * (2 * e + 2))
                for t in range(ST):
                    n = e * ST + t
                    if more:
                        turn(e + 1, t)
                    if t >= 2:
                        pe.wait_ge(o_bias, n - 1)
                    for f in range(KF):
                        if t == 0:
                            pe.wait_ge(h_lo, e * KF + f + 1)
                        for s, r in ((0, 0), (0, 1), (1, 0)):
                            mm = pe.matmul(psO[:, t % 2, :], hT[:, f, s, t * P:(t + 1) * P],
                                           w2s[:, r, f * D:(f + 1) * D],
                                           start=(f + s + r == 0), stop=(f == KF - 1 and s == 1))
                    mm.then_inc(o_done, 1)

            for t in range(ST):
                turn(0, t)
            with pe.Fori(0, E - 1) as e:
                layer_1(e)
                layer_2(e)
            layer_1(E - 1)
            layer_2(E - 1, more=False)


def gated_layer(nc, x, ctx, g_x, g_f, w_sim, b_sim, w_qv, b_qv, w_r, b_r, w1, b1, w2, b2, out):
    x, ctx, out = (a.rearrange("o n d -> (o n) d") for a in (x, ctx, out))
    NI, D = x.shape
    E = w_r.shape[1]
    CAP = max(1, int(1.25 * NI / E))
    ROW = D + 4
    with ExitStack() as st:
        def sbuf(name, shape, dtype):
            return st.enter_context(nc.sbuf_tensor(name, shape, dtype))[:]

        arena = sbuf("arena", [P, 52400], F32)
        cst = {"ident": sbuf("ident", [P, P], F16), "identf": sbuf("identf", [P, P], F32),
               "onesf": sbuf("onesf", [P, P], F32)}
        pooled = sbuf("pooled", [P, 8], F32)
        hc = {"hc": pooled[:, 0:4], "wtot": pooled[:, 4:5], "ctx_inv": pooled[:, 5:6], "ctx_scale": pooled[:, 6:7]}
        ps = st.enter_context(nc.psum_tensor("ps", [P, 8, 512], F32))
        feats = nc.dram_tensor("feats", [NI // 256, P, 3, 2048], F16, kind="Internal").ap()
        rows = nc.dram_tensor("rows", [E * CAP, ROW], F32, kind="Internal").ap()
        attention(nc, ps, arena, cst, x, ctx, w_sim, b_sim, feats, rows, hc)
        ew = ExpertWeights(nc, st, arena, EARLY, w1, b1, w2)
        merge_and_route(nc, ps, arena, cst, x, w_qv, b_qv, g_x, g_f, w_r, b_r, feats, rows, out, hc, ew)
        experts(nc, ps, arena, cst, ew, b2, rows, out)


_INS = ['x', 'ctx_1024', 'g_xattn', 'g_ffn', 'L0_xattn_w_sim', 'L0_xattn_b_sim', 'L0_xattn_W_qv', 'L0_xattn_b_qv',
        'L0_ffn_w_router', 'L0_ffn_b_router', 'L0_ffn_w1', 'L0_ffn_b1', 'L0_ffn_w2', 'L0_ffn_b2']


def kernel(**inputs):
    import numpy as np
    import concourse.bacc as bacc
    from concourse.bass_utils import run_bass_kernel_spmd

    nc = bacc.Bacc("TRN2", target_bir_lowering=False, num_devices=1)
    arrays, args = {}, []
    for name in _INS:
        a = np.ascontiguousarray(inputs[name])
        arrays[f"in_{name}"] = a
        args.append(nc.dram_tensor(f"in_{name}", a.shape, mybir.dt.from_np(a.dtype), kind="ExternalInput").ap())
    out = nc.dram_tensor("out", inputs["x"].shape, F32, kind="ExternalOutput").ap()
    gated_layer(nc, *args, out)
    r = run_bass_kernel_spmd(nc, [arrays], core_ids=[0])
    return r.results[0]["out"]
```
